# Optimizing a Trainium2 kernel written in Bass

```python
import numpy as np
import jax
import jax.numpy as jnp

def _softmax(x, axis=-1):
    return jax.nn.softmax(x, axis=axis)

def _gelu(x):
    return jax.nn.gelu(x, approximate=True)

def _silu(x):
    return jax.nn.silu(x)

def _sigmoid(x):
    return jax.nn.sigmoid(x)

def _layernorm(x, axis=-1, eps=1e-05):
    m = jnp.mean(x, axis=axis, keepdims=True)
    v = jnp.var(x, axis=axis, keepdims=True)
    return (x - m) / jnp.sqrt(v + eps)

def _scatter_add(tgt, idx, src, axis=0):
    return tgt.at[idx].add(src)

def _segment_sum(src, seg, n):
    return jax.ops.segment_sum(src, seg, n)
kernel_name = 'mk_seq_postln_d1_jaxref_r8_65a276'

def setup_inputs(seed: int=0):
    np.random.seed(seed)
    _w = jnp.asarray

    def _L0_attn_setup():
        import jax, jax.numpy as jnp
        import numpy as np
        B_SZ, SEQ, D_MODEL = (2, 64, 128)
        EXPAND, HEAD_DIM = (2, 64)
        D_INNER = EXPAND * D_MODEL
        N_HEADS = D_INNER // HEAD_DIM
        D_STATE = 64
        EPS = 1e-06
        PROJ_DIM = 2 * D_INNER + 2 * N_HEADS * D_STATE + N_HEADS

        def _rope(x, theta):
            x0, x1 = (x[..., 0::2], x[..., 1::2])
            c, s = (jnp.cos(theta), jnp.sin(theta))
            y = jnp.stack([x0 * c - x1 * s, x0 * s + x1 * c], axis=-1)
            return y.reshape(x.shape)
        key = jax.random.key(seed)
        k = jax.random.split(key, 5)
        return {'hidden': jax.random.normal(k[0], (B_SZ, SEQ, D_MODEL), jnp.float32), 'W_in': 0.02 * jax.random.normal(k[1], (D_MODEL, PROJ_DIM), jnp.float32), 'dt_bias': 0.5 * jax.random.normal(k[2], (N_HEADS,), jnp.float32), 'A_log': 0.5 * jax.random.normal(k[3], (N_HEADS,), jnp.float32), 'norm_weight': jnp.ones((D_INNER,), jnp.float32), 'W_out': 0.02 * jax.random.normal(k[4], (D_INNER, D_MODEL), jnp.float32)}
    _L0_attn_in = _L0_attn_setup()

    def _L0_ffn_setup():
        import jax, jax.numpy as jnp
        import numpy as np
        D_MODEL = 128
        D_FF = 512
        N_EXP = 8
        TOP_K = 2

        def _gelu(x):
            return jax.nn.gelu(x, approximate=False)
        key = jax.random.key(seed)
        ks = jax.random.split(key, 12)
        s = 0.02
        return {'x': jax.random.normal(ks[0], (4, 256, D_MODEL), dtype=jnp.float32), 'shared_w1': jax.random.normal(ks[1], (D_MODEL, D_FF), dtype=jnp.float32) * s, 'shared_b1': jnp.zeros((D_FF,), jnp.float32), 'shared_w2': jax.random.normal(ks[2], (D_FF, D_MODEL), dtype=jnp.float32) * s, 'shared_b2': jnp.zeros((D_MODEL,), jnp.float32), 'router_w': jax.random.normal(ks[3], (D_MODEL, N_EXP), dtype=jnp.float32) * s, 'router_b': jnp.zeros((N_EXP,), jnp.float32), 'exp_w1': jax.random.normal(ks[4], (N_EXP, D_MODEL, D_FF), dtype=jnp.float32) * s, 'exp_b1': jnp.zeros((N_EXP, D_FF), jnp.float32), 'exp_w2': jax.random.normal(ks[5], (N_EXP, D_FF, D_MODEL), dtype=jnp.float32) * s, 'exp_b2': jnp.zeros((N_EXP, D_MODEL), jnp.float32)}
    _L0_ffn_in = _L0_ffn_setup()
    _d = {'L0_attn_hidden': _L0_attn_in['hidden'], 'L0_attn_W_in': _L0_attn_in['W_in'], 'L0_attn_dt_bias': _L0_attn_in['dt_bias'], 'L0_attn_A_log': _L0_attn_in['A_log'], 'L0_attn_norm_weight': _L0_attn_in['norm_weight'], 'L0_attn_W_out': _L0_attn_in['W_out'], 'L0_ffn_shared_w1': _L0_ffn_in['shared_w1'], 'L0_ffn_shared_b1': _L0_ffn_in['shared_b1'], 'L0_ffn_shared_w2': _L0_ffn_in['shared_w2'], 'L0_ffn_shared_b2': _L0_ffn_in['shared_b2'], 'L0_ffn_router_w': _L0_ffn_in['router_w'], 'L0_ffn_router_b': _L0_ffn_in['router_b'], 'L0_ffn_exp_w1': _L0_ffn_in['exp_w1'], 'L0_ffn_exp_b1': _L0_ffn_in['exp_b1'], 'L0_ffn_exp_w2': _L0_ffn_in['exp_w2'], 'L0_ffn_exp_b2': _L0_ffn_in['exp_b2']}
    _x0 = _d['L0_attn_hidden']
    _d['L0_attn_hidden'] = jax.random.normal(jax.random.fold_in(jax.random.key(seed), 1), (8, 256, 128), dtype=_x0.dtype)
    del _x0
    return _d

def reference(L0_attn_hidden, L0_attn_W_in, L0_attn_dt_bias, L0_attn_A_log, L0_attn_norm_weight, L0_attn_W_out, L0_ffn_shared_w1, L0_ffn_shared_b1, L0_ffn_shared_w2, L0_ffn_shared_b2, L0_ffn_router_w, L0_ffn_router_b, L0_ffn_exp_w1, L0_ffn_exp_b1, L0_ffn_exp_w2, L0_ffn_exp_b2):

    def _L0_attn_ref(hidden, W_in, dt_bias, A_log, norm_weight, W_out):
        import jax, jax.numpy as jnp
        import numpy as np
        B_SZ, SEQ, D_MODEL = (2, 64, 128)
        EXPAND, HEAD_DIM = (2, 64)
        D_INNER = EXPAND * D_MODEL
        N_HEADS = D_INNER // HEAD_DIM
        D_STATE = 64
        EPS = 1e-06
        PROJ_DIM = 2 * D_INNER + 2 * N_HEADS * D_STATE + N_HEADS

        def _rope(x, theta):
            x0, x1 = (x[..., 0::2], x[..., 1::2])
            c, s = (jnp.cos(theta), jnp.sin(theta))
            y = jnp.stack([x0 * c - x1 * s, x0 * s + x1 * c], axis=-1)
            return y.reshape(x.shape)
        b, l, _ = hidden.shape
        proj = hidden @ W_in
        hn = N_HEADS * D_STATE
        z = proj[..., :D_INNER]
        xr = proj[..., D_INNER:2 * D_INNER].reshape(b, l, N_HEADS, HEAD_DIM)
        Bm = proj[..., 2 * D_INNER:2 * D_INNER + hn].reshape(b, l, N_HEADS, D_STATE)
        Cm = proj[..., 2 * D_INNER + hn:2 * D_INNER + 2 * hn].reshape(b, l, N_HEADS, D_STATE)
        dt = jax.nn.softplus(proj[..., -N_HEADS:] + dt_bias)
        A = -jnp.exp(A_log)
        alpha = jnp.exp(dt * A)
        beta = 0.5 * dt * alpha
        gamma = 0.5 * dt
        half = D_STATE // 2
        inv_freq = 1.0 / 10000.0 ** (jnp.arange(half, dtype=jnp.float32) / half)
        theta = jnp.cumsum(dt, axis=1)[..., None] * inv_freq
        Bm = _rope(Bm, theta)
        Cm = _rope(Cm, theta)
        Bp = jnp.pad(Bm[:, :-1], ((0, 0), (1, 0), (0, 0), (0, 0)))
        xp = jnp.pad(xr[:, :-1], ((0, 0), (1, 0), (0, 0), (0, 0)))
        tl = lambda t: jnp.moveaxis(t, 1, 0)
        xs = (tl(xr), tl(Bm), tl(Cm), tl(Bp), tl(xp), tl(alpha), tl(beta), tl(gamma))
        h0 = jnp.zeros((b, N_HEADS, D_STATE, HEAD_DIM), hidden.dtype)

        def step(h, inp):
            x_t, B_t, C_t, Bprev, xprev, a, bt, g = inp
            h = a[..., None, None] * h + bt[..., None, None] * jnp.einsum('bhn,bhp->bhnp', Bprev, xprev) + g[..., None, None] * jnp.einsum('bhn,bhp->bhnp', B_t, x_t)
            y = jnp.einsum('bhn,bhnp->bhp', C_t, h)
            return (h, y)
        _, ys = jax.lax.scan(step, h0, xs)
        y = jnp.moveaxis(ys, 0, 1).reshape(b, l, D_INNER)
        y = y * jax.nn.silu(z)
        rms = jnp.sqrt(jnp.mean(y * y, axis=-1, keepdims=True) + EPS)
        y = y / rms * norm_weight
        return y @ W_out

    def _L0_ffn_ref(x, shared_w1, shared_b1, shared_w2, shared_b2, router_w, router_b, exp_w1, exp_b1, exp_w2, exp_b2):
        import jax, jax.numpy as jnp
        import numpy as np
        D_MODEL = 128
        D_FF = 512
        N_EXP = 8
        TOP_K = 2

        def _gelu(x):
            return jax.nn.gelu(x, approximate=False)
        leading = x.shape[:-1]
        d = x.shape[-1]
        xf = x.reshape(-1, d)
        T = xf.shape[0]
        h_shared = _gelu(xf @ shared_w1 + shared_b1) @ shared_w2 + shared_b2
        logits = xf @ router_w + router_b
        routing = jax.nn.softmax(logits, axis=-1)
        sel_w, sel_idx = jax.lax.top_k(routing, TOP_K)
        sel_w = sel_w / (jnp.sum(sel_w, axis=-1, keepdims=True) + 1e-09)
        combine = jnp.zeros((T, N_EXP), routing.dtype)
        combine = combine.at[jnp.arange(T)[:, None], sel_idx].add(sel_w)
        residual = jnp.zeros_like(xf)
        for e in range(N_EXP):
            h = _gelu(xf @ exp_w1[e] + exp_b1[e])
            y = h @ exp_w2[e] + exp_b2[e]
            residual = residual + combine[:, e:e + 1] * y
        out = h_shared + residual
        return out.reshape(*leading, d)
    x = L0_attn_hidden
    x = _layernorm(x + _L0_attn_ref(x, L0_attn_W_in, L0_attn_dt_bias, L0_attn_A_log, L0_attn_norm_weight, L0_attn_W_out), axis=-1)
    x = _layernorm(x + _L0_ffn_ref(x, L0_ffn_shared_w1, L0_ffn_shared_b1, L0_ffn_shared_w2, L0_ffn_shared_b2, L0_ffn_router_w, L0_ffn_router_b, L0_ffn_exp_w1, L0_ffn_exp_b1, L0_ffn_exp_w2, L0_ffn_exp_b2), axis=-1)
    return x

_drawn_inputs = setup_inputs


def setup_inputs(seed=0):
    import zlib

    import numpy as np

    out = dict(_drawn_inputs(seed))
    spreads = {'L0_attn_norm_weight': (1.0, 0.2),
     'L0_ffn_shared_b1': (0.0, 0.362),
     'L0_ffn_shared_b2': (0.0, 0.1),
     'L0_ffn_router_b': (0.0, 0.1),
     'L0_ffn_exp_b1': (0.0, 0.486),
     'L0_ffn_exp_b2': (0.0, 0.1)}
    factors = {}
    for name, (base, spread) in spreads.items():
        noise = np.random.default_rng([zlib.crc32(name.encode()), seed]).standard_normal(out[name].shape)
        drawn = base * np.exp(spread * noise) if base else spread * noise
        out[name] = jnp.asarray(drawn.astype(out[name].dtype))
    for name, factor in factors.items():
        out[name] = (out[name] * factor).astype(out[name].dtype)
    return out
```

```python
from contextlib import ExitStack

import numpy as np

import concourse.bass as bass
from concourse import mybir

ALU = mybir.AluOpType
ACT = mybir.ActivationFunctionType
F32 = mybir.dt.float32
AX_X = mybir.AxisListType.X

P = 128
NSEQ, L = 8, 256
T = NSEQ * L
NT = T // P
H, HD = 4, 64
HALF = 32
DI = H * HD
FF, NE = 512, 8
FC = FF // P
CH = 512
NCH = T // CH
Z0, X0, B0, C0, DT0 = 0, DI, 2 * DI, 3 * DI, 4 * DI
RMS_EPS, LN_EPS = 1e-6, 1e-5
MAGIC = 12582912.0
TURN = 6.283185005187988
FAR = 1e30


def build(nc, hidden, w_in, w_dt, dt_bias, a_log, norm_w, w_out, inv_freq, w1, w2,
          router_w, router_b, comb_dram, out):
    ctx = ExitStack()
    with ctx:
        def sb(name, shape, dt=F32):
            return ctx.enter_context(nc.sbuf_tensor(name, shape, dt))

        def sem(name):
            return ctx.enter_context(nc.semaphore(name))

        hid = sb("hid", [P, NT, P])
        hidT = sb("hidT", [P, T])
        win = sb("win", [P, 4 * DI + H])
        wdt = sb("wdt", [P, P])
        wout = sb("wout", [P, 2, P])
        vecs = sb("vecs", [P, 16])
        half = sb("half", [P, 4])
        epsr = sb("epsr", [P, 2])
        epsl = sb("epsl", [P, 4])
        rw = sb("rw", [P, NE])
        rb = sb("rb", [P, NE])
        ident = sb("ident", [P, P])
        sel = sb("sel", [P, H, P])
        ones = sb("ones", [P, L])
        dt = sb("dt", [P, T])
        cum = sb("cum", [P, T])
        cosT = sb("cosT", [P, T])
        sinT = sb("sinT", [P, T])
        sc1 = sb("sc1", [P, T])
        sc2 = sb("sc2", [P, T])
        cumK = sb("cumK", [P, NT, H])
        dtK = sb("dtK", [P, NT, H])
        gK = sb("gK", [P, NT, H])
        gx = sb("gx", [P, NT, H])
        nratio = sb("nratio", [P, NT, H])
        hTb = sb("hTb", [P, L])
        th = sb("th", [P, 2, DI])
        szr = sb("szr", [P, 4, DI])
        xs = sb("xs", [P, 4, DI])
        U = sb("U", [P, 4, L])
        V = sb("V", [P, 4, L])
        R = sb("R", [P, 4, L])
        Bm = sb("Bm", [P, H, 2, L])
        D = sb("D", [P, H, 3, P])
        E = sb("E", [P, H, 3, P])
        DI0 = sb("DI0", [P, 2, H, P])
        Pm = sb("Pm", [P, H, 3, P])
        yg = sb("yg", [P, 2, DI])
        sq = sb("sq", [P, DI])
        ssq = sb("ssq", [P, 2])
        rms = sb("rms", [P, 2])
        yT = sb("yT", [P, 2, 2, P])
        x1p = sb("x1p", [P, 2, P])
        st = sb("st", [P, 2, 6])
        mv = sb("mv", [P, 2, 2])
        rstd = sb("rstd", [P, 2])
        x1 = sb("x1", [P, 2, P])
        x1Tb = sb("x1Tb", [P, L])
        x1T = sb("x1T", [P, T])
        logits = sb("logits", [P, NT, NE])
        rt = sb("rt", [P, 8, NT, NE])
        rs = sb("rs", [P, 8, NT])
        iota8 = sb("iota8", [P, NT, NE])
        combT = sb("combT", [P, P])
        w1r = sb("w1r", [P, 2, FF + FC + 1])
        w2r = sb("w2r", [P, 2, FC, P])
        tmp = sb("tmp", [P, 2, CH])
        fst = sb("fst", [P, 4, 6])
        fmv = sb("fmv", [P, 4, 2])
        frs = sb("frs", [P, 4])
        outb = sb("outb", [P, NT, P])
        cbc = [cosT, sinT]
        g = [sc1, sc2]
        acc = dt

        ps = ctx.enter_context(nc.psum_tensor("ps", [P, 8, 512], F32))
        Zb = ps[:, 0, :]
        BCb = ps[:, 1:3, :].rearrange("p a b -> p (a b)").rearrange("p (f t) -> p f t", t=L)
        S0b = ps[:, 3:5, :].rearrange("p a b -> p (a b)").rearrange("p (h t) -> p h t", t=L)
        S1b = ps[:, 5, :].rearrange("p (h t) -> p h t", t=P)
        Yb = ps[:, 6, :].rearrange("p (j f) -> p j f", j=2)
        Mb = ps[:, 7, :]
        dtb = ps[:, 4:8, :].rearrange("p a b -> p (a b)")

        s_hid = [sem(f"s_hid{q}") for q in range(4)]
        s_w = sem("s_w")
        s_vec = sem("s_vec")
        s_rw = sem("s_rw")
        s_cst = sem("s_cst")
        s_id = sem("s_id")
        s_hT = sem("s_hT")
        s_hTc = sem("s_hTc")
        s_dtp = sem("s_dtp")
        s_abs = sem("s_abs")
        s_A = sem("s_A")
        s_Aneg = sem("s_Aneg")
        s_wo = sem("s_wo")
        s_mx = sem("s_mx")
        s_dt = sem("s_dt")
        s_gs = sem("s_gs")
        s_cum = sem("s_cum")
        s_tab = sem("s_tab")
        s_absr = sem("s_absr")
        s_cos = sem("s_cos")
        s_sin = sem("s_sin")
        s_tk = sem("s_tk")
        s_tkc = sem("s_tkc")
        s_rat = sem("s_rat")
        s_hTb = sem("s_hTb")
        s_zx = sem("s_zx")
        s_th = sem("s_th")
        s_xs = sem("s_xs")
        s_sz = sem("s_sz")
        s_bc = sem("s_bc")
        s_uv = sem("s_uv")
        s_rope = sem("s_rope")
        s_bm = sem("s_bm")
        s_cb = sem("s_cb")
        s_D = sem("s_D")
        s_Dm = sem("s_Dm")
        s_di = sem("s_di")
        s_E = sem("s_E")
        s_Em = sem("s_Em")
        s_S = sem("s_S")
        s_P = sem("s_P")
        s_pv = sem("s_pv")
        s_yg = sem("s_yg")
        s_ssq = sem("s_ssq")
        s_rm = sem("s_rm")
        s_yT = sem("s_yT")
        s_yTc = sem("s_yTc")
        s_o = sem("s_o")
        s_x1p = sem("s_x1p")
        s_st = sem("s_st")
        s_mv = sem("s_mv")
        s_rstd = sem("s_rstd")
        s_x1 = sem("s_x1")
        s_x1T = sem("s_x1T")
        s_x1Tb = sem("s_x1Tb")
        s_x1Tc = sem("s_x1Tc")
        s_lg = sem("s_lg")
        s_lgc = sem("s_lgc")
        s_rt = sem("s_rt")
        s_rte = sem("s_rte")
        s_cT = sem("s_cT")
        s_cTc = sem("s_cTc")
        s_cd = sem("s_cd")
        s_cbc = [sem(f"s_cbc{q}") for q in range(2)]
        s_we = [sem(f"s_we{q}") for q in range(2)]
        s_h = sem("s_h")
        s_g = sem("s_g")
        s_O = sem("s_O")
        s_ob = sem("s_ob")
        s_acc = sem("s_acc")
        s_ft = sem("s_ft")
        s_fst = sem("s_fst")
        s_fmv = sem("s_fmv")
        s_frs = sem("s_frs")
        s_fin = sem("s_fin")
        s_out = sem("s_out")

        block = ctx.enter_context(nc.Block())

        NVEC = 8

        @block.sync
        def _(sp):
            hv = hidden.rearrange("(n p) d -> p n d", p=P)
            for q in range(4):
                sp.dma_start(hid[:, 4 * q:4 * q + 4, :], hv[:, 4 * q:4 * q + 4, :]).then_inc(s_hid[q], 16)

            def load_expert(e, slot):
                sp.dma_start(w1r[:, slot, :], w1[e]).then_inc(s_we[slot], 16)
                sp.dma_start(w2r[:, slot, :, :], w2[e].rearrange("(c p) d -> p c d", p=P)).then_inc(s_we[slot], 16)

            def load_combine(e, slot):
                src = comb_dram.rearrange("(n e) t -> e n t", e=NE)[e]
                sp.dma_start(cbc[slot][:, :].rearrange("p (n t) -> p n t", t=P),
                             src[None, :, :].broadcast_to([P, NT, P])).then_inc(s_cbc[slot], 16)

            load_expert(0, 0)
            load_expert(1, 1)
            sp.wait_ge(s_cTc, 1)
            sp.dma_start(comb_dram, combT[:, :]).then_inc(s_cd, 16)
            sp.wait_ge(s_cd, 16)
            load_combine(0, 0)
            load_combine(1, 1)
            with sp.Fori(1, NE // 2) as k:
                for slot in range(2):
                    sp.wait_ge(s_acc, 8 * k + 4 * slot - 4)
                    load_expert(2 * k + slot, slot)
                    load_combine(2 * k + slot, slot)
            sp.wait_ge(s_acc, 4 * (NE - 1))
            load_expert(NE, 0)
            ov = out.rearrange("(n p) d -> p n d", p=P)
            for c in range(NCH):
                sp.wait_ge(s_fin, 4 * (c + 1))
                sp.dma_start(ov[:, 4 * c:4 * c + 4, :], outb[:, 4 * c:4 * c + 4, :]).then_inc(s_out, 16)
            sp.wait_ge(s_out, 16 * NCH)

        @block.gpsimd
        def _(pool):
            gp = nc.gpsimd
            gp.memset(ident[:, :], 0.0).then_inc(s_cst, 1)
            gp.memset(sel[:, :, :], 0.0).then_inc(s_cst, 1)
            pool.wait_ge(s_cst, 2)
            gp.affine_select(out=ident[:, :], in_=ident[:, :], compare_op=ALU.not_equal, fill=1.0,
                             base=0, pattern=[[-1, P]], channel_multiplier=1).then_inc(s_id, 1)
            gp.affine_select(out=sel[:, :, :], in_=sel[:, :, :], compare_op=ALU.not_equal, fill=1.0,
                             base=0, pattern=[[-HALF, H], [0, P]], channel_multiplier=1).then_inc(s_id, 1)
            gp.memset(ones[:, :], 1.0).then_inc(s_cst, 1)
            gp.memset(half[:, :], -0.5).then_inc(s_cst, 1)
            gp.memset(epsr[:, :], RMS_EPS).then_inc(s_cst, 1)
            gp.memset(epsl[:, :], LN_EPS).then_inc(s_cst, 1)
            gp.memset(Bm[:, :, :, :], 0.0).then_inc(s_cst, 1)
            gp.iota(iota8[:, :, :], pattern=[[0, NT], [1, NE]], base=0, channel_multiplier=0,
                    allow_small_or_imprecise_dtypes=True).then_inc(s_cst, 1)
            pool.wait_ge(s_dt, 4)
            gp.tensor_copy(sc1[:, T - 1:T], dt[:, T - 1:T]).then_inc(s_gs, 1)
            gp.tensor_tensor(sc1[:, 0:T - 1], dt[:, 0:T - 1], dt[:, 1:T], ALU.add).then_inc(s_gs, 1)

            def rotate(b):
                pool.wait_ge(s_uv, 2 * b + 2)
                if not isinstance(b, int) or b > 0:
                    pool.wait_ge(s_S, b)
                    pool.wait_ge(s_bm, 4 * b)
                gp.tensor_tensor(R[:, 0::2, :], U[:, 0::2, :], V[:, 1::2, :], ALU.subtract).then_inc(s_rope, 1)
                gp.tensor_tensor(R[:, 1::2, :], V[:, 0::2, :], U[:, 1::2, :], ALU.add).then_inc(s_rope, 1)

            def distances(b):
                for j in range(2):
                    if j == 1:
                        pool.wait_ge(s_D, 2 * b + 2)
                    elif not isinstance(b, int) or b > 0:
                        pool.wait_ge(s_Em, 2 * b)
                    else:
                        pool.wait_ge(s_rat, 5)
                    gp.tensor_tensor(DI0[:, j, :, :], ident[:, :].rearrange("p (o t) -> p o t", o=1).broadcast_to([P, H, P]),
                                     nratio[:, bass.ds(2 * b + j, 1), :].rearrange("p o h -> p h o").broadcast_to([P, H, P]),
                                     ALU.mult).then_inc(s_di, 1)
                for j in range(2):
                    gp.affine_select(out=D[:, :, 2 * j, :], in_=D[:, :, 2 * j, :], compare_op=ALU.is_ge,
                                     fill=FAR, base=0, pattern=[[0, H], [1, P]],
                                     channel_multiplier=-1).then_inc(s_Dm, 1)

            def diagonal(b):
                pool.wait_ge(s_E, 4 * b + 4)
                pool.wait_ge(s_di, 2 * b + 2)
                for j in range(2):
                    gp.tensor_tensor(E[:, :, 2 * j, :], E[:, :, 2 * j, :], DI0[:, j, :, :],
                                     ALU.subtract).then_inc(s_Em, 1)

            def rms_rows(b):
                pool.wait_ge(s_ssq, 2 * b + 2)
                if not isinstance(b, int) or b > 0:
                    pool.wait_ge(s_x1p, 2 * b)
                gp.tensor_tensor(rms[:, :], ssq[:, :], epsr[:, :], ALU.add).then_inc(s_rm, 1)
                pool.wait_ge(s_rm, 2 * b + 1)
                gp.tensor_tensor(rms[:, :], rms[:, :], half[:, 0:2], ALU.pow).then_inc(s_rm, 1)

            def ln_rows(b):
                pool.wait_ge(s_mv, 2 * b + 2)
                if not isinstance(b, int) or b > 0:
                    pool.wait_ge(s_x1, 2 * b)
                gp.tensor_tensor(rstd[:, :], mv[:, :, 1], epsl[:, 0:2], ALU.add).then_inc(s_rstd, 1)
                pool.wait_ge(s_rstd, 2 * b + 1)
                gp.tensor_tensor(rstd[:, :], rstd[:, :], half[:, 0:2], ALU.pow).then_inc(s_rstd, 1)

            def step(k, now=True, nxt=True, last=True):
                if last:
                    rms_rows(k - 1)
                if now:
                    distances(k)
                if last:
                    ln_rows(k - 1)
                if now:
                    diagonal(k)
                if nxt:
                    rotate(k + 1)

            steps(pool, step)

            for c in range(NCH):
                pool.wait_ge(s_fmv, 4 * c + 4)
                if c > 0:
                    pool.wait_ge(s_fin, 4 * c)
                gp.tensor_tensor(frs[:, :], fmv[:, :, 1], epsl[:, :], ALU.add).then_inc(s_frs, 1)
                pool.wait_ge(s_frs, 2 * c + 1)
                gp.tensor_tensor(frs[:, :], frs[:, :], half[:, :], ALU.pow).then_inc(s_frs, 1)

        @block.scalar
        def _(act):
            ac = nc.scalar
            act.dma_start(wdt[:, :], w_dt).then_inc(s_w, 16)
            act.dma_start(win[:, :], w_in).then_inc(s_w, 16)
            act.dma_start(vecs[:, 0:1], dt_bias).then_inc(s_vec, 16)
            act.dma_start(vecs[:, 1:2], inv_freq).then_inc(s_vec, 16)
            act.dma_start(vecs[:, 2:6], a_log).then_inc(s_vec, 16)
            act.dma_start(vecs[:, 6:8], norm_w).then_inc(s_vec, 16)
            act.dma_start(wout[:, :, :], w_out.rearrange("(c p) d -> p c d", p=P)).then_inc(s_vec, 16)
            act.dma_start(rw[:, :], router_w).then_inc(s_rw, 16)
            act.dma_start(rb[:, :], router_b).then_inc(s_rw, 16)
            act.wait_ge(s_vec, 80)
            ac.activation(vecs[:, 8:12], vecs[:, 2:6], ACT.Exp).then_inc(s_A, 1)
            act.wait_ge(s_dtp, 4)
            ac.activation(sc1[:, :], dtb, ACT.Abs, bias=vecs[:, 0:1]).then_inc(s_abs, 1)
            act.wait_ge(s_abs, 1)
            ac.activation(sc2[:, :], sc1[:, :], ACT.Exp, scale=-1.0).then_inc(s_abs, 1)
            act.wait_ge(s_abs, 2)
            for q in range(4):
                ac.activation(sc2[:, q * 512:(q + 1) * 512], sc2[:, q * 512:(q + 1) * 512], ACT.Ln,
                              bias=1.0).then_inc(s_abs, 1)
            act.wait_ge(s_tab, 3)
            ac.activation(sinT[:, :], sc2[:, :], ACT.Sin, scale=-TURN).then_inc(s_sin, 1)
            ac.activation(cosT[:, :], sc2[:, :], ACT.Abs).then_inc(s_absr, 1)
            act.wait_ge(s_absr, 1)
            act.wait_ge(s_Aneg, 2)
            ac.activation(cosT[:, :], cosT[:, :], ACT.Sin, scale=-TURN, bias=vecs[:, 12:13]).then_inc(s_cos, 1)

            def next_tile(b):
                if not isinstance(b, int) or b > 0:
                    act.wait_ge(s_zx, 2 * b)
                    act.wait_ge(s_bc, b)
                ac.copy(hTb[:, :], hidT[:, bass.ts(b, L)]).then_inc(s_hTb, 1)

            def gate(b):
                for j in range(2):
                    act.wait_ge(s_zx, 2 * b + j + 1)
                    if not isinstance(b, int) or b > 0:
                        act.wait_ge(s_sz, 2 * b + j - 1)
                    ac.activation(th[:, j, :], Zb[:, 0:DI], ACT.Tanh, scale=0.5).then_inc(s_th, 1)

            def mask(b):
                act.wait_ge(s_rope, 2 * b + 2)
                if not isinstance(b, int) or b > 0:
                    act.wait_ge(s_S, b)
                else:
                    act.wait_ge(s_cst, 7)
                for h in range(H):
                    rows = slice(HALF * h, HALF * h + HALF)
                    ac.copy(Bm[rows, h, :, :], R[rows, 0:2, :]).then_inc(s_bm, 1)

            def exponentials(b):
                act.wait_ge(s_Dm, 2 * b + 2)
                if not isinstance(b, int) or b > 0:
                    act.wait_ge(s_P, 2 * b)
                for h in range(H):
                    ac.activation(E[:, h, :, :], D[:, h, :, :], ACT.Exp, scale=vecs[:, 2 + h:3 + h]).then_inc(s_E, 1)

            def squares(b):
                act.wait_ge(s_yg, b + 1)
                if not isinstance(b, int) or b > 0:
                    act.wait_ge(s_rm, 2 * b)
                for j in range(2):
                    ac.activation(sq[:, :], yg[:, j, :], ACT.Square, scale=DI ** -0.5, accum_out=ssq[:, j:j + 1]).then_inc(s_ssq, 1)
                    act.wait_ge(s_ssq, 2 * b + j + 1)

            def copy_yT(b):
                act.wait_ge(s_yT, b + 1)
                ac.copy(yT[:, :, :, :].rearrange("p j c t -> p (j c t)"), Mb).then_inc(s_yTc, 1)

            def copy_x1T(b):
                act.wait_ge(s_x1T, b + 1)
                ac.copy(x1Tb[:, :], Mb[:, 0:L]).then_inc(s_x1Tb, 1)
                act.wait_ge(s_x1Tb, b + 1)
                ac.copy(x1T[:, bass.ts(b, L)], x1Tb[:, :]).then_inc(s_x1Tc, 1)

            def step(k, now=True, nxt=True, last=True):
                if last:
                    squares(k - 1)
                    copy_yT(k - 1)
                if nxt:
                    next_tile(k + 1)
                    gate(k + 1)
                if now:
                    exponentials(k)
                if last:
                    copy_x1T(k - 1)
                if nxt:
                    mask(k + 1)

            steps(act, step)

            act.wait_ge(s_rt, 7)
            ac.activation(rt[:, 2, :, :], rt[:, 1, :, :], ACT.Exp).then_inc(s_rte, 1)

            def gelu(u, slot, par):
                for f in range(FC):
                    act.wait_ge(s_h, 4 * u + f + 1)
                    ac.activation(g[par][:, f * CH:(f + 1) * CH], ps[:, f, :], ACT.Gelu,
                                  bias=w1r[:, slot, FF + f:FF + f + 1]).then_inc(s_g, 1)

            with act.Fori(0, NE // 2) as k:
                for j in range(8):
                    gelu(8 * k + j, j // 4, j % 2)
            for j in range(4):
                gelu(4 * NE + j, 0, j % 2)

        @block.vector
        def _(dve):
            v = nc.vector
            for q in range(4):
                dve.wait_ge(s_hT, q + 1)
                v.tensor_copy(hidT[:, 512 * q:512 * q + 512], ps[:, q, :]).then_inc(s_hTc, 1)
            dve.wait_ge(s_vec, 80)
            dve.wait_ge(s_A, 1)
            v.tensor_scalar(vecs[:, 2:6], vecs[:, 8:12], -1.0, None, ALU.mult).then_inc(s_Aneg, 1)
            v.memset(vecs[:, 12:13], float(np.pi / 2)).then_inc(s_Aneg, 1)
            for c in range(2):
                v.tensor_scalar(wout[:, c, :], wout[:, c, :], vecs[:, 6 + c:7 + c], None, ALU.mult).then_inc(s_wo, 1)
            dve.wait_ge(s_abs, 1)
            v.tensor_scalar(dt[:, :], dtb, vecs[:, 0:1], 0.0, ALU.add, ALU.max).then_inc(s_mx, 1)
            dve.wait_ge(s_mx, 1)
            for q in range(4):
                dve.wait_ge(s_abs, 3 + q)
                w = slice(q * 512, (q + 1) * 512)
                v.tensor_tensor(dt[:, w], dt[:, w], sc2[:, w], ALU.add).then_inc(s_dt, 1)
            dve.wait_ge(s_cst, 3)
            for b in range(NSEQ):
                dve.wait_ge(s_dt, b // 2 + 1)
                w = slice(b * L, (b + 1) * L)
                v.tensor_tensor_scan(cum[:, w], ones[:, :], dt[:, w], 0.0, ALU.mult, ALU.add).then_inc(s_cum, 1)
            dve.wait_ge(s_cum, NSEQ)
            v.tensor_scalar(sinT[:, :], cum[:, :], vecs[:, 1:2], float(1 / (2 * np.pi)), ALU.mult, ALU.mult).then_inc(s_tab, 1)
            dve.wait_ge(s_tab, 1)
            v.tensor_scalar(cosT[:, :], sinT[:, :], MAGIC, None, ALU.add).then_inc(s_tab, 1)
            dve.wait_ge(s_tab, 2)
            v.scalar_tensor_tensor(out=sc2[:, :], in0=cosT[:, :], scalar=MAGIC, in1=sinT[:, :],
                                   op0=ALU.subtract, op1=ALU.subtract).then_inc(s_tab, 1)
            for n, dst in enumerate((cumK, dtK, gK)):
                for q in range(4):
                    dve.wait_ge(s_tk, 4 * n + q + 1)
                    v.tensor_copy(dst[:, 4 * q:4 * q + 4, :],
                                  ps[:, q, :].rearrange("p (n h i) -> p n h i", h=H, i=HALF)[:, :, :, 0]).then_inc(s_tkc, 1)
            dve.wait_ge(s_tkc, 12)
            v.tensor_scalar(gK[:, :, :], gK[:, :, :], 1e-30, None, ALU.max).then_inc(s_rat, 1)
            dve.wait_ge(s_rat, 1)
            v.tensor_scalar(gx[:, :, :], gK[:, :, :], 0.25, None, ALU.mult).then_inc(s_rat, 1)
            v.reciprocal(nratio[:, :, :], gK[:, :, :]).then_inc(s_rat, 1)
            dve.wait_ge(s_rat, 3)
            v.tensor_tensor(nratio[:, :, :], nratio[:, :, :], dtK[:, :, :], ALU.mult).then_inc(s_rat, 1)
            dve.wait_ge(s_rat, 4)
            v.tensor_scalar(nratio[:, :, :], nratio[:, :, :], -1.0, 1.0, ALU.mult, ALU.add).then_inc(s_rat, 1)

            def bcast(ap, n):
                return ap.rearrange("p o h -> p h o").broadcast_to([P, H, n])

            def gate(b):
                ring = 2 * (b % 2)
                for j in range(2):
                    dve.wait_ge(s_th, 2 * b + j + 1)
                    if not isinstance(b, int) or b > 1:
                        dve.wait_ge(s_pv, b - 1)
                        dve.wait_ge(s_yg, b - 1)
                    v.tensor_tensor(xs[:, bass.ds(ring + j, 1), :].rearrange("p o (h d) -> p (o h) d", h=H),
                                    Zb[:, DI:2 * DI].rearrange("p (h d) -> p h d", h=H),
                                    bcast(gx[:, bass.ds(2 * b + j, 1), :], HD), ALU.mult).then_inc(s_xs, 1)
                    v.scalar_tensor_tensor(out=szr[:, bass.ds(ring + j, 1), :].rearrange("p o d -> p (o d)"),
                                           in0=th[:, j, :], scalar=1.0,
                                           in1=Zb[:, 0:DI], op0=ALU.add, op1=ALU.mult).then_inc(s_sz, 1)

            def turn(b):
                dve.wait_ge(s_bc, b + 1)
                if not isinstance(b, int) or b > 0:
                    dve.wait_ge(s_rope, 2 * b)
                else:
                    dve.wait_ge(s_cos, 1)
                    dve.wait_ge(s_sin, 1)
                for tab, dst in ((cosT, U), (sinT, V)):
                    v.tensor_tensor(dst[:, :, :], BCb, tab[:, bass.ts(b, L)].rearrange("p (o t) -> p o t", o=1)
                                    .broadcast_to([P, 4, L]), ALU.mult).then_inc(s_uv, 1)

            def distances(b):
                dve.wait_ge(s_cb, b + 1)
                if not isinstance(b, int) or b > 0:
                    dve.wait_ge(s_E, 4 * b)
                v.tensor_tensor(D[:, :, 0:2, :].rearrange("p h a t -> p h (a t)"), BCb, bcast(cumK[:, bass.ds(2 * b, 1), :], L),
                                ALU.subtract).then_inc(s_D, 1)
                v.tensor_tensor(D[:, :, 2, :], BCb[:, :, P:L], bcast(cumK[:, bass.ds(2 * b + 1, 1), :], P),
                                ALU.subtract).then_inc(s_D, 1)

            def weigh(b):
                dve.wait_ge(s_S, b + 1)
                dve.wait_ge(s_Em, 2 * b + 2)
                if not isinstance(b, int) or b > 0:
                    dve.wait_ge(s_pv, b)
                v.tensor_tensor(Pm[:, :, 0:2, :].rearrange("p h a t -> p h (a t)"), S0b,
                                E[:, :, 0:2, :].rearrange("p h a t -> p h (a t)"), ALU.mult).then_inc(s_P, 1)
                v.tensor_tensor(Pm[:, :, 2, :], S1b, E[:, :, 2, :], ALU.mult).then_inc(s_P, 1)

            def gated(b):
                dve.wait_ge(s_pv, b + 1)
                dve.wait_ge(s_sz, 2 * b + 2)
                if not isinstance(b, int) or b > 0:
                    dve.wait_ge(s_yT, b)
                    dve.wait_ge(s_ssq, 2 * b)
                v.tensor_tensor(yg[:, :, :], Yb, szr[:, bass.ds(2 * (b % 2), 2), :], ALU.mult).then_inc(s_yg, 1)

            def norm(b):
                dve.wait_ge(s_o, b + 1)
                dve.wait_ge(s_rm, 2 * b + 2)
                for j in range(2):
                    v.scalar_tensor_tensor(out=x1p[:, j, :], in0=Mb[:, j * P:(j + 1) * P], scalar=rms[:, j:j + 1],
                                           in1=hid[:, bass.ds(2 * b + j, 1), :].rearrange("p o d -> p (o d)"),
                                           op0=ALU.mult, op1=ALU.add).then_inc(s_x1p, 1)
                for j in range(2):
                    dve.wait_ge(s_x1p, 2 * b + j + 1)
                    v.bn_stats(st[:, j, :], x1p[:, j, :]).then_inc(s_st, 1)
                for j in range(2):
                    dve.wait_ge(s_rw, 32)
                    dve.wait_ge(s_st, 2 * b + j + 1)
                    v.bn_aggr(mv[:, j, :], st[:, j, :]).then_inc(s_mv, 1)

            def norm_out(b):
                dve.wait_ge(s_rstd, 2 * b + 2)
                if not isinstance(b, int) or b > 0:
                    dve.wait_ge(s_x1T, b)
                for j in range(2):
                    v.tensor_scalar(x1[:, j, :], x1p[:, j, :], mv[:, j, 0:1], rstd[:, j:j + 1],
                                    ALU.subtract, ALU.mult).then_inc(s_x1, 1)

            def keep_logits(b):
                dve.wait_ge(s_lg, b + 1)
                v.tensor_tensor(logits[:, bass.ds(2 * b, 2), :], Mb[:, L:L + 2 * NE].rearrange("p (j e) -> p j e", j=2),
                                rb[:, :].rearrange("p (o e) -> p o e", o=1).broadcast_to([P, 2, NE]),
                                ALU.add).then_inc(s_lgc, 1)

            def step(k, now=True, nxt=True, last=True):
                if now:
                    distances(k)
                if nxt:
                    gate(k + 1)
                if last:
                    norm(k - 1)
                if now:
                    weigh(k)
                if last:
                    norm_out(k - 1)
                if nxt:
                    turn(k + 1)
                if last:
                    keep_logits(k - 1)
                if now:
                    gated(k)

            dve.wait_ge(s_rw, 32)
            steps(dve, step)

            n = [0]

            def did(ins):
                n[0] += 1
                ins.then_inc(s_rt, 1)

            def rowb(i):
                return rs[:, i, :].rearrange("p (n o) -> p n o", o=1).broadcast_to([P, NT, NE])

            dve.wait_ge(s_lgc, NSEQ)
            dve.wait_ge(s_cst, 8)
            v.tensor_reduce(rs[:, 0, :], logits[:, :, :], AX_X, ALU.max).then_inc(s_rt, 1)
            dve.wait_ge(s_rt, 1)
            v.tensor_tensor(rt[:, 1, :, :], logits[:, :, :], rowb(0), ALU.subtract).then_inc(s_rt, 1)
            dve.wait_ge(s_rt, 2)
            v.tensor_scalar(rt[:, 3, :, :], iota8[:, :, :], float(NE), None, ALU.subtract).then_inc(s_rt, 1)
            v.tensor_scalar(rt[:, 4, :, :], rt[:, 1, :, :], 0.0, None, ALU.is_equal).then_inc(s_rt, 1)
            dve.wait_ge(s_rt, 4)
            v.tensor_tensor(rt[:, 5, :, :], rt[:, 4, :, :], rt[:, 3, :, :], ALU.mult).then_inc(s_rt, 1)
            dve.wait_ge(s_rt, 5)
            v.tensor_reduce(rs[:, 1, :], rt[:, 5, :, :], AX_X, ALU.min).then_inc(s_rt, 1)
            dve.wait_ge(s_rt, 6)
            v.tensor_tensor(rt[:, 4, :, :], rt[:, 3, :, :], rowb(1), ALU.is_equal).then_inc(s_rt, 1)
            dve.wait_ge(s_rt, 7)
            v.scalar_tensor_tensor(out=rt[:, 5, :, :], in0=rt[:, 4, :, :], scalar=-3e38, in1=rt[:, 1, :, :],
                                   op0=ALU.mult, op1=ALU.add).then_inc(s_rt, 1)
            dve.wait_ge(s_rt, 8)
            v.tensor_reduce(rs[:, 2, :], rt[:, 5, :, :], AX_X, ALU.max).then_inc(s_rt, 1)
            dve.wait_ge(s_rt, 9)
            v.tensor_tensor(rt[:, 6, :, :], rt[:, 5, :, :], rowb(2), ALU.is_equal).then_inc(s_rt, 1)
            dve.wait_ge(s_rt, 10)
            v.tensor_tensor(rt[:, 6, :, :], rt[:, 6, :, :], rt[:, 3, :, :], ALU.mult).then_inc(s_rt, 1)
            dve.wait_ge(s_rt, 11)
            v.tensor_reduce(rs[:, 3, :], rt[:, 6, :, :], AX_X, ALU.min).then_inc(s_rt, 1)
            dve.wait_ge(s_rt, 12)
            v.tensor_tensor(rt[:, 6, :, :], rt[:, 3, :, :], rowb(3), ALU.is_equal).then_inc(s_rt, 1)
            dve.wait_ge(s_rt, 13)
            v.tensor_tensor(rt[:, 4, :, :], rt[:, 4, :, :], rt[:, 6, :, :], ALU.add).then_inc(s_rt, 1)
            dve.wait_ge(s_rte, 1)
            v.tensor_reduce(rs[:, 4, :], rt[:, 2, :, :], AX_X, ALU.add).then_inc(s_rt, 1)
            dve.wait_ge(s_rt, 15)
            v.reciprocal(rs[:, 5, :], rs[:, 4, :]).then_inc(s_rt, 1)
            v.tensor_tensor(rt[:, 4, :, :], rt[:, 4, :, :], rt[:, 2, :, :], ALU.mult).then_inc(s_rt, 1)
            dve.wait_ge(s_rt, 17)
            v.tensor_tensor(rt[:, 4, :, :], rt[:, 4, :, :], rowb(5), ALU.mult).then_inc(s_rt, 1)
            dve.wait_ge(s_rt, 18)
            v.tensor_reduce(rs[:, 6, :], rt[:, 4, :, :], AX_X, ALU.add).then_inc(s_rt, 1)
            dve.wait_ge(s_rt, 19)
            v.tensor_scalar(rs[:, 6, :], rs[:, 6, :], 1e-9, None, ALU.add).then_inc(s_rt, 1)
            dve.wait_ge(s_rt, 20)
            v.reciprocal(rs[:, 7, :], rs[:, 6, :]).then_inc(s_rt, 1)
            dve.wait_ge(s_rt, 21)
            v.tensor_tensor(rt[:, 7, :, :], rt[:, 4, :, :], rowb(7), ALU.mult).then_inc(s_rt, 1)
            dve.wait_ge(s_cT, 1)
            v.tensor_copy(combT[:, :], ps[:, 6, 0:P]).then_inc(s_cTc, 1)

            dve.wait_ge(s_x1Tc, NSEQ)
            v.tensor_copy(acc[:, :], x1T[:, :]).then_inc(s_ob, 2)
            dve.wait_ge(s_ob, 2)

            def add_unit(u, k, slot, c, first):
                w = slice(c * CH, (c + 1) * CH)
                if c == 0:
                    dve.wait_ge(s_cbc[slot], 16 * k + 16)
                dve.wait_ge(s_O, u + 1)
                v.scalar_tensor_tensor(out=tmp[:, c % 2, :], in0=ps[:, 4 + c % 2, :], scalar=w1r[:, slot, FF + FC:FF + FC + 1],
                                       in1=cbc[slot][:, w], op0=ALU.add, op1=ALU.mult).then_inc(s_ob, 1)
                dve.wait_ge(s_ob, u + 3)
                v.tensor_tensor(acc[:, w], acc[:, w], tmp[:, c % 2, :], ALU.add).then_inc(s_acc, 1)

            with dve.Fori(0, NE // 2) as k:
                for j in range(8):
                    add_unit(8 * k + j, k, j // 4, j % 4, False)

            def finish(c):
                for q in range(4):
                    dve.wait_ge(s_ft, c + 1)
                    v.bn_stats(fst[:, q, :], ps[:, 6 + c % 2, q * P:(q + 1) * P]).then_inc(s_fst, 1)
                for q in range(4):
                    dve.wait_ge(s_fst, 4 * c + q + 1)
                    v.bn_aggr(fmv[:, q, :], fst[:, q, :]).then_inc(s_fmv, 1)
                dve.wait_ge(s_frs, 2 * c + 2)
                for q in range(4):
                    v.tensor_scalar(outb[:, 4 * c + q, :], ps[:, 6 + c % 2, q * P:(q + 1) * P], fmv[:, q, 0:1],
                                    frs[:, q:q + 1], ALU.subtract, ALU.mult).then_inc(s_fin, 1)

            for c in range(NCH):
                w = slice(c * CH, (c + 1) * CH)
                u = 4 * NE + c
                dve.wait_ge(s_O, u + 1)
                v.scalar_tensor_tensor(out=acc[:, w], in0=ps[:, 4 + c % 2, :], scalar=w1r[:, 0, FF + FC:FF + FC + 1],
                                       in1=acc[:, w], op0=ALU.add, op1=ALU.add).then_inc(s_acc, 1)
                if c > 0:
                    finish(c - 1)
            finish(NCH - 1)

        @block.tensor
        def _(pe):
            te = nc.tensor
            pe.wait_ge(s_id, 1)
            for q in range(4):
                pe.wait_ge(s_hid[q], 16)
                for j in range(4):
                    m = te.transpose(ps[:, q, j * P:(j + 1) * P], hid[:, 4 * q + j, :], ident[:, :])
                m.then_inc(s_hT, 1)
            pe.wait_ge(s_w, 32)
            for q in range(4):
                pe.wait_ge(s_hTc, q + 1)
                te.matmul(ps[:, 4 + q, :], wdt[:, :], hidT[:, 512 * q:512 * q + 512], start=True,
                          stop=True).then_inc(s_dtp, 1)
            for n, src in enumerate((cum, dt, sc1)):
                if n == 0:
                    pe.wait_ge(s_cum, NSEQ)
                if n == 2:
                    pe.wait_ge(s_gs, 2)
                for q in range(4):
                    if n > 0:
                        pe.wait_ge(s_tkc, 4 * (n - 1) + q + 1)
                    for j in range(4):
                        t0 = (4 * q + j) * P
                        m = te.transpose(ps[:, q, j * P:(j + 1) * P], src[:, t0:t0 + P], ident[:, :])
                    m.then_inc(s_tk, 1)

            def spread(b):
                pe.wait_ge(s_uv, 2 * b + 2)
                for h in range(H):
                    m = te.matmul(BCb[:, h, :], sel[:, h, :], cum[:, bass.ts(b, L)], start=True, stop=True)
                m.then_inc(s_cb, 1)

            def scores(b):
                pe.wait_ge(s_bm, 4 * b + 4)
                pe.wait_ge(s_rope, 2 * b + 2)
                if not isinstance(b, int) or b > 0:
                    pe.wait_ge(s_P, 2 * b)
                for h in range(H):
                    for e in range(2):
                        te.matmul(S0b[:, h, :], Bm[:, h, e, 0:P], R[:, 2 + e, :], start=(e == 0), stop=(e == 1))
                for h in range(H):
                    for e in range(2):
                        m = te.matmul(S1b[:, h, :], Bm[:, h, e, P:L], R[:, 2 + e, P:L], start=(e == 0), stop=(e == 1))
                m.then_inc(s_S, 1)

            def project_zx(b):
                pe.wait_ge(s_hTb, b + 1)
                for j in range(2):
                    if not isinstance(b, int) or b > 0 or j > 0:
                        pe.wait_ge(s_sz, 2 * b + j)
                    te.matmul(Zb, hTb[:, j * P:(j + 1) * P], win[:, Z0:B0], start=True, stop=True).then_inc(s_zx, 1)

            def project_bc(b):
                if not isinstance(b, int) or b > 0:
                    pe.wait_ge(s_D, 2 * b)
                for n, c0 in enumerate((B0, B0 + 1, C0, C0 + 1)):
                    m = te.matmul(BCb[:, n, :], win[:, c0:c0 + DI - 1:2], hTb[:, :], start=True, stop=True)
                m.then_inc(s_bc, 1)

            def values(b):
                pe.wait_ge(s_P, 2 * b + 2)
                pe.wait_ge(s_xs, 2 * b + 2)
                if not isinstance(b, int) or b > 0:
                    pe.wait_ge(s_yg, b)
                ring = 2 * (b % 2)
                for h in range(H):
                    f = slice(h * HD, (h + 1) * HD)
                    x0 = xs[:, bass.ds(ring, 1), f].rearrange("p o d -> p (o d)")
                    x1_ = xs[:, bass.ds(ring + 1, 1), f].rearrange("p o d -> p (o d)")
                    te.matmul(Yb[:, 0, f], Pm[:, h, 0, :], x0, start=True, stop=True)
                    te.matmul(Yb[:, 1, f], Pm[:, h, 1, :], x0, start=True, stop=False)
                    m = te.matmul(Yb[:, 1, f], Pm[:, h, 2, :], x1_, start=False, stop=True)
                m.then_inc(s_pv, 1)

            def turn_y(b):
                pe.wait_ge(s_yg, b + 1)
                if not isinstance(b, int) or b > 0:
                    pe.wait_ge(s_lgc, b)
                for j in range(2):
                    for c in range(2):
                        n = 2 * j + c
                        m = te.transpose(Mb[:, n * P:(n + 1) * P], yg[:, j, c * P:(c + 1) * P], ident[:, :])
                m.then_inc(s_yT, 1)

            def project_out(b):
                pe.wait_ge(s_yTc, b + 1)
                if isinstance(b, int) and b == 0:
                    pe.wait_ge(s_wo, 2)
                for j in range(2):
                    for c in range(2):
                        m = te.matmul(Mb[:, j * P:(j + 1) * P], yT[:, j, c, :], wout[:, c, :], start=(c == 0), stop=(c == 1))
                m.then_inc(s_o, 1)

            def turn_x1(b):
                pe.wait_ge(s_x1, 2 * b + 2)
                for j in range(2):
                    m = te.transpose(Mb[:, j * P:(j + 1) * P], x1[:, j, :], ident[:, :])
                m.then_inc(s_x1T, 1)

            def route(b):
                pe.wait_ge(s_x1Tb, b + 1)
                for j in range(2):
                    m = te.matmul(Mb[:, L + j * NE:L + (j + 1) * NE], x1Tb[:, j * P:(j + 1) * P], rw[:, :], start=True, stop=True)
                m.then_inc(s_lg, 1)

            def step(k, now=True, nxt=True, last=True):
                if last:
                    turn_y(k - 1)
                if now:
                    spread(k)
                if last:
                    project_out(k - 1)
                if nxt:
                    project_zx(k + 1)
                if now:
                    scores(k)
                if last:
                    turn_x1(k - 1)
                if nxt:
                    project_bc(k + 1)
                if last:
                    route(k - 1)
                if now:
                    values(k)

            pe.wait_ge(s_id, 2)
            pe.wait_ge(s_rw, 32)
            pe.wait_ge(s_tkc, 12)
            pe.wait_ge(s_mx, 1)
            steps(pe, step)

            pe.wait_ge(s_rt, 22)
            te.transpose(ps[:, 6, 0:P], rt[:, 7, :, :].rearrange("p n e -> p (n e)"), ident[:, :]).then_inc(s_cT, 1)
            pe.wait_ge(s_ob, 2)

            def first(u, slot, count, c, start):
                if c == 0:
                    pe.wait_ge(s_we[slot], count)
                for f in range(FC):
                    if not start:
                        pe.wait_ge(s_g, 4 * u + f - 3)
                    te.matmul(ps[:, f, :], w1r[:, slot, f * P:(f + 1) * P], x1T[:, c * CH:(c + 1) * CH],
                              start=True, stop=True).then_inc(s_h, 1)

            def second(u, slot, par):
                pe.wait_ge(s_ob, u + 1)
                for f in range(FC):
                    pe.wait_ge(s_g, 4 * u + f + 1)
                    m = te.matmul(ps[:, 4 + par, :], w2r[:, slot, f, :], g[par][:, f * CH:(f + 1) * CH],
                                  start=(f == 0), stop=(f == FC - 1))
                m.then_inc(s_O, 1)

            first(0, 0, 32, 0, True)
            with pe.Fori(0, NE // 2) as k:
                for j in range(8):
                    n = j + 1
                    first(8 * k + n, n // 4 % 2, 32 * k + 32 * (1 + n // 8), n % 4, False)
                    second(8 * k + j, j // 4, j % 2)

            def turn_out(c):
                pe.wait_ge(s_acc, 4 * NE + c + 1)
                if c >= 2:
                    pe.wait_ge(s_fin, 4 * (c - 1))
                for q in range(4):
                    t0 = c * CH + q * P
                    m = te.transpose(ps[:, 6 + c % 2, q * P:(q + 1) * P], acc[:, t0:t0 + P], ident[:, :])
                m.then_inc(s_ft, 1)

            for c in range(NCH):
                if c + 1 < NCH:
                    first(4 * NE + c + 1, 0, 0, c + 1, False)
                if c < 2:
                    pe.wait_ge(s_ob, 4 * NE + c + 1)
                else:
                    pe.wait_ge(s_acc, 4 * NE + c - 1)
                for f in range(FC):
                    pe.wait_ge(s_g, 4 * (4 * NE + c) + f + 1)
                    m = te.matmul(ps[:, 4 + c % 2, :], w2r[:, 0, f, :], g[c % 2][:, f * CH:(f + 1) * CH],
                                  start=(f == 0), stop=(f == FC - 1))
                m.then_inc(s_O, 1)
                if c > 0:
                    turn_out(c - 1)
            turn_out(NCH - 1)


def steps(engine, step):
    step(-1, now=False, last=False)
    step(0, last=False)
    with engine.Fori(1, NSEQ - 1) as k:
        step(k)
    step(NSEQ - 1, nxt=False)
    step(NSEQ, now=False, nxt=False)


def kernel(**inputs):
    import concourse.bacc as _bacc
    from concourse.bass_utils import run_bass_kernel_spmd as _run

    a = {k: np.asarray(v) for k, v in inputs.items()}
    at, ff = "L0_attn_", "L0_ffn_"
    w_in = a[at + "W_in"]
    half = np.arange(HALF, dtype=np.float32) / np.float32(HALF)
    inv = (np.float32(1.0) / np.power(np.float32(10000.0), half)).astype(np.float32)
    arrays = {
        "hidden": a[at + "hidden"].reshape(T, P),
        "w_in": w_in,
        "w_dt": np.repeat(w_in[:, DT0:DT0 + H], HALF, axis=1),
        "dt_bias": np.repeat(a[at + "dt_bias"], HALF).reshape(P, 1),
        "a_log": np.broadcast_to(a[at + "A_log"][None, :], (P, H)),
        "norm_w": a[at + "norm_weight"].reshape(2, P).T,
        "w_out": a[at + "W_out"],
        "inv_freq": np.tile(inv, H).reshape(P, 1),
        "w1": np.concatenate([
            np.concatenate([a[ff + "exp_w1"], a[ff + "shared_w1"][None]], axis=0),
            np.concatenate([a[ff + "exp_b1"], a[ff + "shared_b1"][None]], axis=0).reshape(NE + 1, FC, P).transpose(0, 2, 1),
            np.concatenate([a[ff + "exp_b2"], a[ff + "shared_b2"][None]], axis=0)[:, :, None]], axis=2),
        "w2": np.concatenate([a[ff + "exp_w2"], a[ff + "shared_w2"][None]], axis=0),
        "router_w": a[ff + "router_w"],
        "router_b": np.broadcast_to(a[ff + "router_b"][None, :], (P, NE)),
    }
    nc = _bacc.Bacc("TRN2", target_bir_lowering=False, num_devices=1)
    feed, args = {}, []
    for name, x in arrays.items():
        x = np.ascontiguousarray(x)
        feed[f"in_{name}"] = x
        args.append(nc.dram_tensor(f"in_{name}", x.shape, mybir.dt.from_np(x.dtype), kind="ExternalInput").ap())
    comb = nc.dram_tensor("comb_dram", (NT * NE, P), F32, kind="Internal").ap()
    out = nc.dram_tensor("out_0", (T, P), F32, kind="ExternalOutput").ap()
    build(nc, *args, comb, out)
    r = _run(nc, [feed], core_ids=[0])
    return r.results[0]["out_0"].reshape(NSEQ, L, P)
```

```python
from contextlib import ExitStack

import numpy as np

import concourse.bass as bass
from concourse import mybir

ALU = mybir.AluOpType
ACT = mybir.ActivationFunctionType
F32 = mybir.dt.float32
F16 = mybir.dt.float16
AX_X = mybir.AxisListType.X

P = 128
NSEQ, L = 8, 256
T = NSEQ * L
NT = T // P
H, HD = 4, 64
HALF = 32
DI = H * HD
FF, NE = 512, 8
FC = FF // P
CH = 512
NCH = T // CH
Z0, X0, B0, C0, DT0 = 0, DI, 2 * DI, 3 * DI, 4 * DI
RMS_EPS, LN_EPS = 1e-6, 1e-5
MAGIC = 12582912.0
TURN = 6.283185005187988
WS = 256.0
FAR = 1e30


def build(nc, hidden, w_in, w_dt, dt_bias, a_log, norm_w, w_out, inv_freq, w1, w2,
          router_w, router_b, comb_dram, out):
    ctx = ExitStack()
    with ctx:
        def sb(name, shape, dt=F32):
            return ctx.enter_context(nc.sbuf_tensor(name, shape, dt))

        def sem(name):
            return ctx.enter_context(nc.semaphore(name))

        hid = sb("hid", [P, NT, P])
        hidT = sb("hidT", [P, T])
        win = sb("win", [P, 4 * DI + H])
        wdt = sb("wdt", [P, P])
        wout = sb("wout", [P, 2, P])
        vecs = sb("vecs", [P, 16])
        half = sb("half", [P, 4])
        epsr = sb("epsr", [P, 2])
        epsl = sb("epsl", [P, 4])
        rw = sb("rw", [P, NE])
        rb = sb("rb", [P, NE])
        ident = sb("ident", [P, P])
        sel = sb("sel", [P, H, P])
        ones = sb("ones", [P, L])
        dt = sb("dt", [P, T])
        cum = sb("cum", [P, T])
        cosT = sb("cosT", [P, T])
        sinT = sb("sinT", [P, T])
        sc1 = sb("sc1", [P, T])
        sc2 = sb("sc2", [P, T])
        cumK = sb("cumK", [P, NT, H])
        dtK = sb("dtK", [P, NT, H])
        gK = sb("gK", [P, NT, H])
        gx = sb("gx", [P, NT, H])
        nratio = sb("nratio", [P, NT, H])
        hTb = sb("hTb", [P, L])
        th = sb("th", [P, 2, DI])
        szr = sb("szr", [P, 4, DI])
        xs = sb("xs", [P, 4, DI])
        U = sb("U", [P, 4, L])
        V = sb("V", [P, 4, L])
        R = sb("R", [P, 4, L])
        Bm = sb("Bm", [P, H, 2, L])
        D = sb("D", [P, H, 3, P])
        E = sb("E", [P, H, 3, P])
        DI0 = sb("DI0", [P, 2, H, P])
        Pm = sb("Pm", [P, H, 3, P])
        yg = sb("yg", [P, 2, DI])
        sq = sb("sq", [P, DI])
        ssq = sb("ssq", [P, 2])
        rms = sb("rms", [P, 2])
        yT = sb("yT", [P, 2, 2, P])
        x1p = sb("x1p", [P, 2, P])
        st = sb("st", [P, 2, 6])
        mv = sb("mv", [P, 2, 2])
        rstd = sb("rstd", [P, 2])
        x1 = sb("x1", [P, 2, P])
        x1Tb = sb("x1Tb", [P, L])
        acc = sb("acc", [P, T])
        x1h = sb("x1h", [P, T], F16)
        x1l = sb("x1l", [P, T], F16)
        logits = sb("logits", [P, NT, NE])
        rt = sb("rt", [P, 8, NT, NE])
        rs = sb("rs", [P, 8, NT])
        iota8 = sb("iota8", [P, NT, NE])
        combT = sb("combT", [P, P])
        w1r = sb("w1r", [P, 2, FF + FC + 1])
        w2r = sb("w2r", [P, 2, FC * P])
        b1s = sb("b1s", [P, 2, FC])
        b2s = sb("b2s", [P, 2])
        w1h = sb("w1h", [P, 2, FF], F16)
        w1l = sb("w1l", [P, 2, FF], F16)
        w2h = sb("w2h", [P, 2, FC * P], F16)
        w2l = sb("w2l", [P, 2, FC * P], F16)
        gh = sb("gh", [P, 2, FC * CH], F16)
        gl = sb("gl", [P, 2, FC * CH], F16)
        tmp = sb("tmp", [P, 2, CH])
        fst = sb("fst", [P, 4, 6])
        fmv = sb("fmv", [P, 4, 2])
        frs = sb("frs", [P, 4])
        outb = sb("outb", [P, NT, P])
        cbc = [cosT, sinT]
        g = [sc1, sc2]

        ps = ctx.enter_context(nc.psum_tensor("ps", [P, 8, 512], F32))
        Zb = ps[:, 0, :]
        BCb = ps[:, 1:3, :].rearrange("p a b -> p (a b)").rearrange("p (f t) -> p f t", t=L)
        S0b = ps[:, 3:5, :].rearrange("p a b -> p (a b)").rearrange("p (h t) -> p h t", t=L)
        S1b = ps[:, 5, :].rearrange("p (h t) -> p h t", t=P)
        Yb = ps[:, 6, :].rearrange("p (j f) -> p j f", j=2)
        Mb = ps[:, 7, :]
        dtb = ps[:, 4:8, :].rearrange("p a b -> p (a b)")

        s_hid = [sem(f"s_hid{q}") for q in range(4)]
        s_w = sem("s_w")
        s_vec = sem("s_vec")
        s_rw = sem("s_rw")
        s_cst = sem("s_cst")
        s_id = sem("s_id")
        s_hT = sem("s_hT")
        s_hTc = sem("s_hTc")
        s_dtp = sem("s_dtp")
        s_abs = sem("s_abs")
        s_A = sem("s_A")
        s_Aneg = sem("s_Aneg")
        s_wo = sem("s_wo")
        s_mx = sem("s_mx")
        s_dt = sem("s_dt")
        s_gs = sem("s_gs")
        s_cum = sem("s_cum")
        s_tab = sem("s_tab")
        s_absr = sem("s_absr")
        s_cos = sem("s_cos")
        s_sin = sem("s_sin")
        s_tk = sem("s_tk")
        s_tkc = sem("s_tkc")
        s_rat = sem("s_rat")
        s_hTb = sem("s_hTb")
        s_zx = sem("s_zx")
        s_th = sem("s_th")
        s_xs = sem("s_xs")
        s_sz = sem("s_sz")
        s_bc = sem("s_bc")
        s_uv = sem("s_uv")
        s_rope = sem("s_rope")
        s_bm = sem("s_bm")
        s_cb = sem("s_cb")
        s_D = sem("s_D")
        s_Dm = sem("s_Dm")
        s_di = sem("s_di")
        s_E = sem("s_E")
        s_Em = sem("s_Em")
        s_S = sem("s_S")
        s_P = sem("s_P")
        s_pv = sem("s_pv")
        s_yg = sem("s_yg")
        s_ssq = sem("s_ssq")
        s_rm = sem("s_rm")
        s_yT = sem("s_yT")
        s_yTc = sem("s_yTc")
        s_o = sem("s_o")
        s_x1p = sem("s_x1p")
        s_st = sem("s_st")
        s_mv = sem("s_mv")
        s_rstd = sem("s_rstd")
        s_x1 = sem("s_x1")
        s_x1T = sem("s_x1T")
        s_x1Tb = sem("s_x1Tb")
        s_x1a = sem("s_x1a")
        s_x1h = sem("s_x1h")
        s_x1l = sem("s_x1l")
        s_lg = sem("s_lg")
        s_lgc = sem("s_lgc")
        s_rt = sem("s_rt")
        s_rte = sem("s_rte")
        s_cT = sem("s_cT")
        s_cTc = sem("s_cTc")
        s_cd = sem("s_cd")
        s_cbc = [sem(f"s_cbc{q}") for q in range(2)]
        s_we = [sem(f"s_we{q}") for q in range(2)]
        s_h = sem("s_h")
        s_g = sem("s_g")
        s_gh = sem("s_gh")
        s_gl = sem("s_gl")
        s_wh = sem("s_wh")
        s_wl = sem("s_wl")
        s_O = sem("s_O")
        s_ob = sem("s_ob")
        s_acc = sem("s_acc")
        s_ft = sem("s_ft")
        s_fst = sem("s_fst")
        s_fmv = sem("s_fmv")
        s_frs = sem("s_frs")
        s_fin = sem("s_fin")
        s_out = sem("s_out")

        block = ctx.enter_context(nc.Block())

        NVEC = 8

        @block.sync
        def _(sp):
            hv = hidden.rearrange("(n p) d -> p n d", p=P)
            for q in range(4):
                sp.dma_start(hid[:, 4 * q:4 * q + 4, :], hv[:, 4 * q:4 * q + 4, :]).then_inc(s_hid[q], 16)

            def load_expert(e, slot):
                sp.dma_start(w1r[:, slot, :], w1[e]).then_inc(s_we[slot], 16)
                sp.dma_start(w2r[:, slot, :].rearrange("p (c d) -> p c d", c=FC), w2[e].rearrange("(c p) d -> p c d", p=P)).then_inc(s_we[slot], 16)

            def load_combine(e, slot):
                src = comb_dram.rearrange("(n e) t -> e n t", e=NE)[e]
                sp.dma_start(cbc[slot][:, :].rearrange("p (n t) -> p n t", t=P),
                             src[None, :, :].broadcast_to([P, NT, P])).then_inc(s_cbc[slot], 16)

            load_expert(0, 0)
            load_expert(1, 1)
            sp.wait_ge(s_cTc, 1)
            sp.dma_start(comb_dram, combT[:, :]).then_inc(s_cd, 16)
            sp.wait_ge(s_cd, 16)
            load_combine(0, 0)
            load_combine(1, 1)
            with sp.Fori(1, NE // 2) as k:
                for slot in range(2):
                    sp.wait_ge(s_wl, 8 * k + 4 * slot - 4)
                    load_expert(2 * k + slot, slot)
                    sp.wait_ge(s_acc, 8 * k + 4 * slot - 4)
                    load_combine(2 * k + slot, slot)
            sp.wait_ge(s_wl, 4 * (NE - 1))
            load_expert(NE, 0)
            ov = out.rearrange("(n p) d -> p n d", p=P)
            for c in range(NCH):
                sp.wait_ge(s_fin, 4 * (c + 1))
                sp.dma_start(ov[:, 4 * c:4 * c + 4, :], outb[:, 4 * c:4 * c + 4, :]).then_inc(s_out, 16)
            sp.wait_ge(s_out, 16 * NCH)

        @block.gpsimd
        def _(pool):
            gp = nc.gpsimd
            gp.memset(ident[:, :], 0.0).then_inc(s_cst, 1)
            gp.memset(sel[:, :, :], 0.0).then_inc(s_cst, 1)
            pool.wait_ge(s_cst, 2)
            gp.affine_select(out=ident[:, :], in_=ident[:, :], compare_op=ALU.not_equal, fill=1.0,
                             base=0, pattern=[[-1, P]], channel_multiplier=1).then_inc(s_id, 1)
            gp.affine_select(out=sel[:, :, :], in_=sel[:, :, :], compare_op=ALU.not_equal, fill=1.0,
                             base=0, pattern=[[-HALF, H], [0, P]], channel_multiplier=1).then_inc(s_id, 1)
            gp.memset(ones[:, :], 1.0).then_inc(s_cst, 1)
            gp.memset(half[:, :], -0.5).then_inc(s_cst, 1)
            gp.memset(epsr[:, :], RMS_EPS).then_inc(s_cst, 1)
            gp.memset(epsl[:, :], LN_EPS).then_inc(s_cst, 1)
            gp.memset(Bm[:, :, :, :], 0.0).then_inc(s_cst, 1)
            gp.iota(iota8[:, :, :], pattern=[[0, NT], [1, NE]], base=0, channel_multiplier=0,
                    allow_small_or_imprecise_dtypes=True).then_inc(s_cst, 1)
            pool.wait_ge(s_dt, 4)
            gp.tensor_copy(sc1[:, T - 1:T], dt[:, T - 1:T]).then_inc(s_gs, 1)
            gp.tensor_tensor(sc1[:, 0:T - 1], dt[:, 0:T - 1], dt[:, 1:T], ALU.add).then_inc(s_gs, 1)

            def rotate(b):
                pool.wait_ge(s_uv, 2 * b + 2)
                if not isinstance(b, int) or b > 0:
                    pool.wait_ge(s_S, b)
                    pool.wait_ge(s_bm, 4 * b)
                gp.tensor_tensor(R[:, 0::2, :], U[:, 0::2, :], V[:, 1::2, :], ALU.subtract).then_inc(s_rope, 1)
                gp.tensor_tensor(R[:, 1::2, :], V[:, 0::2, :], U[:, 1::2, :], ALU.add).then_inc(s_rope, 1)

            def distances(b):
                for j in range(2):
                    if j == 1:
                        pool.wait_ge(s_D, 2 * b + 2)
                    elif not isinstance(b, int) or b > 0:
                        pool.wait_ge(s_Em, 2 * b)
                    else:
                        pool.wait_ge(s_rat, 5)
                    gp.tensor_tensor(DI0[:, j, :, :], ident[:, :].rearrange("p (o t) -> p o t", o=1).broadcast_to([P, H, P]),
                                     nratio[:, bass.ds(2 * b + j, 1), :].rearrange("p o h -> p h o").broadcast_to([P, H, P]),
                                     ALU.mult).then_inc(s_di, 1)
                for j in range(2):
                    gp.affine_select(out=D[:, :, 2 * j, :], in_=D[:, :, 2 * j, :], compare_op=ALU.is_ge,
                                     fill=FAR, base=0, pattern=[[0, H], [1, P]],
                                     channel_multiplier=-1).then_inc(s_Dm, 1)

            def diagonal(b):
                pool.wait_ge(s_E, 4 * b + 4)
                pool.wait_ge(s_di, 2 * b + 2)
                for j in range(2):
                    gp.tensor_tensor(E[:, :, 2 * j, :], E[:, :, 2 * j, :], DI0[:, j, :, :],
                                     ALU.subtract).then_inc(s_Em, 1)

            def rms_rows(b):
                pool.wait_ge(s_ssq, 2 * b + 2)
                if not isinstance(b, int) or b > 0:
                    pool.wait_ge(s_x1p, 2 * b)
                gp.tensor_tensor(rms[:, :], ssq[:, :], epsr[:, :], ALU.add).then_inc(s_rm, 1)
                pool.wait_ge(s_rm, 2 * b + 1)
                gp.tensor_tensor(rms[:, :], rms[:, :], half[:, 0:2], ALU.pow).then_inc(s_rm, 1)

            def ln_rows(b):
                pool.wait_ge(s_mv, 2 * b + 2)
                if not isinstance(b, int) or b > 0:
                    pool.wait_ge(s_x1, 2 * b)
                gp.tensor_tensor(rstd[:, :], mv[:, :, 1], epsl[:, 0:2], ALU.add).then_inc(s_rstd, 1)
                pool.wait_ge(s_rstd, 2 * b + 1)
                gp.tensor_tensor(rstd[:, :], rstd[:, :], half[:, 0:2], ALU.pow).then_inc(s_rstd, 1)

            def low_part(b):
                pool.wait_ge(s_x1h, b + 1)
                gp.tensor_tensor(x1l[:, bass.ts(b, L)], x1Tb[:, :], x1h[:, bass.ts(b, L)], ALU.subtract).then_inc(s_x1l, 1)

            def step(k):
                if live(k, -1):
                    rms_rows(k - 1)
                if live(k, 1):
                    rotate(k + 1)
                    distances(k + 1)
                if live(k, -1):
                    ln_rows(k - 1)
                if live(k, 1):
                    diagonal(k + 1)
                if live(k, -1):
                    low_part(k - 1)

            steps(pool, step)

            for c in range(NCH):
                pool.wait_ge(s_fmv, 4 * c + 4)
                if c > 0:
                    pool.wait_ge(s_fin, 4 * c)
                gp.tensor_tensor(frs[:, :], fmv[:, :, 1], epsl[:, :], ALU.add).then_inc(s_frs, 1)
                pool.wait_ge(s_frs, 2 * c + 1)
                gp.tensor_tensor(frs[:, :], frs[:, :], half[:, :], ALU.pow).then_inc(s_frs, 1)

        @block.scalar
        def _(act):
            ac = nc.scalar
            act.dma_start(wdt[:, :], w_dt).then_inc(s_w, 16)
            act.dma_start(win[:, :], w_in).then_inc(s_w, 16)
            act.dma_start(vecs[:, 0:1], dt_bias).then_inc(s_vec, 16)
            act.dma_start(vecs[:, 1:2], inv_freq).then_inc(s_vec, 16)
            act.dma_start(vecs[:, 2:6], a_log).then_inc(s_vec, 16)
            act.dma_start(vecs[:, 6:8], norm_w).then_inc(s_vec, 16)
            act.dma_start(wout[:, :, :], w_out.rearrange("(c p) d -> p c d", p=P)).then_inc(s_vec, 16)
            act.dma_start(rw[:, :], router_w).then_inc(s_rw, 16)
            act.dma_start(rb[:, :], router_b).then_inc(s_rw, 16)
            act.wait_ge(s_vec, 80)
            ac.activation(vecs[:, 8:12], vecs[:, 2:6], ACT.Exp).then_inc(s_A, 1)
            act.wait_ge(s_dtp, 4)
            ac.activation(sc1[:, :], dtb, ACT.Abs, bias=vecs[:, 0:1]).then_inc(s_abs, 1)
            act.wait_ge(s_abs, 1)
            ac.activation(sc2[:, :], sc1[:, :], ACT.Exp, scale=-1.0).then_inc(s_abs, 1)
            act.wait_ge(s_abs, 2)
            for q in range(4):
                ac.activation(sc2[:, q * 512:(q + 1) * 512], sc2[:, q * 512:(q + 1) * 512], ACT.Ln,
                              bias=1.0).then_inc(s_abs, 1)
            act.wait_ge(s_tab, 3)
            ac.activation(sinT[:, :], sc2[:, :], ACT.Sin, scale=-TURN).then_inc(s_sin, 1)
            ac.activation(cosT[:, :], sc2[:, :], ACT.Abs).then_inc(s_absr, 1)
            act.wait_ge(s_absr, 1)
            act.wait_ge(s_Aneg, 2)
            ac.activation(cosT[:, :], cosT[:, :], ACT.Sin, scale=-TURN, bias=vecs[:, 12:13]).then_inc(s_cos, 1)

            def next_tile(b):
                if not isinstance(b, int) or b > 0:
                    act.wait_ge(s_zx, 2 * b)
                    act.wait_ge(s_bc, b)
                ac.copy(hTb[:, :], hidT[:, bass.ts(b, L)]).then_inc(s_hTb, 1)

            def gate(b, j):
                act.wait_ge(s_zx, 2 * b + j + 1)
                if not isinstance(b, int) or b > 0:
                    act.wait_ge(s_sz, 2 * b + j - 1)
                ac.activation(th[:, j, :], Zb[:, 0:DI], ACT.Tanh, scale=0.5).then_inc(s_th, 1)

            def mask(b):
                act.wait_ge(s_rope, 2 * b + 2)
                if not isinstance(b, int) or b > 0:
                    act.wait_ge(s_S, b)
                else:
                    act.wait_ge(s_cst, 7)
                for h in range(H):
                    rows = slice(HALF * h, HALF * h + HALF)
                    ac.copy(Bm[rows, h, :, :], R[rows, 0:2, :]).then_inc(s_bm, 1)

            def exponentials(b):
                act.wait_ge(s_Dm, 2 * b + 2)
                if not isinstance(b, int) or b > 0:
                    act.wait_ge(s_P, 2 * b)
                for h in range(H):
                    ac.activation(E[:, h, :, :], D[:, h, :, :], ACT.Exp, scale=vecs[:, 2 + h:3 + h]).then_inc(s_E, 1)

            def squares(b):
                act.wait_ge(s_yg, b + 1)
                if not isinstance(b, int) or b > 0:
                    act.wait_ge(s_rm, 2 * b)
                for j in range(2):
                    ac.activation(sq[:, :], yg[:, j, :], ACT.Square, scale=DI ** -0.5, accum_out=ssq[:, j:j + 1]).then_inc(s_ssq, 1)
                    act.wait_ge(s_ssq, 2 * b + j + 1)

            def copy_yT(b):
                act.wait_ge(s_yT, b + 1)
                ac.copy(yT[:, :, :, :].rearrange("p j c t -> p (j c t)"), Mb).then_inc(s_yTc, 1)

            def copy_x1T(b):
                act.wait_ge(s_x1T, b + 1)
                if not isinstance(b, int) or b > 0:
                    act.wait_ge(s_x1l, b)
                ac.copy(x1Tb[:, :], Mb[:, 0:L]).then_inc(s_x1Tb, 1)
                act.wait_ge(s_x1Tb, b + 1)
                ac.copy(x1h[:, bass.ts(b, L)], x1Tb[:, :]).then_inc(s_x1h, 1)
                ac.copy(acc[:, bass.ts(b, L)], x1Tb[:, :]).then_inc(s_x1a, 1)

            def step(k):
                if live(k, 1):
                    next_tile(k + 1)
                if live(k, -1):
                    squares(k - 1)
                    copy_yT(k - 1)
                if live(k, 1):
                    gate(k + 1, 0)
                    mask(k + 1)
                    gate(k + 1, 1)
                    exponentials(k + 1)
                if live(k, -1):
                    copy_x1T(k - 1)

            steps(act, step)

            def split_high(e, slot, count):
                act.wait_ge(s_we[slot], count)
                if not isinstance(e, int) or e > 1:
                    act.wait_ge(s_O, 4 * e - 4)
                ac.mul(w1h[:, slot, :], w1r[:, slot, 0:FF], WS).then_inc(s_wh, 1)
                ac.mul(w2h[:, slot, :], w2r[:, slot, :], WS).then_inc(s_wh, 1)

            split_high(0, 0, 32)
            split_high(1, 1, 32)
            act.wait_ge(s_rt, 7)
            ac.activation(rt[:, 2, :, :], rt[:, 1, :, :], ACT.Exp).then_inc(s_rte, 1)

            def gelu(u, slot, par, first=False):
                for f in range(FC):
                    if not first and f == 0:
                        act.wait_ge(s_gl, 2 * u - 2)
                    act.wait_ge(s_h, 4 * u + f + 1)
                    ac.activation(g[par][:, f * CH:(f + 1) * CH], ps[:, f, :], ACT.Gelu, scale=1.0 / WS,
                                  bias=b1s[:, slot, f:f + 1]).then_inc(s_g, 1)
                for q in range(2):
                    if not first and q == 0:
                        act.wait_ge(s_O, u - 1)
                    act.wait_ge(s_g, 4 * u + 2 * q + 2)
                    w = slice(2 * q * CH, 2 * (q + 1) * CH)
                    ac.copy(gh[:, par, w], g[par][:, w]).then_inc(s_gh, 1)

            for j in range(8):
                gelu(j, j // 4, j % 2, first=j < 2)
                if j == 5:
                    split_high(2, 0, 64)
            with act.Fori(1, NE // 2) as k:
                for j in range(8):
                    gelu(8 * k + j, j // 4, j % 2)
                    if j == 1:
                        split_high(2 * k + 1, 1, 32 * k + 32)
                    if j == 5:
                        split_high(2 * k + 2, 0, 32 * k + 64)
            for j in range(4):
                gelu(4 * NE + j, 0, j % 2)

        @block.vector
        def _(dve):
            v = nc.vector
            for q in range(4):
                dve.wait_ge(s_hT, q + 1)
                v.tensor_copy(hidT[:, 512 * q:512 * q + 512], ps[:, q, :]).then_inc(s_hTc, 1)
            dve.wait_ge(s_vec, 80)
            dve.wait_ge(s_A, 1)
            v.tensor_scalar(vecs[:, 2:6], vecs[:, 8:12], -1.0, None, ALU.mult).then_inc(s_Aneg, 1)
            v.memset(vecs[:, 12:13], float(np.pi / 2)).then_inc(s_Aneg, 1)
            for c in range(2):
                v.tensor_scalar(wout[:, c, :], wout[:, c, :], vecs[:, 6 + c:7 + c], None, ALU.mult).then_inc(s_wo, 1)
            dve.wait_ge(s_abs, 1)
            v.tensor_scalar(dt[:, :], dtb, vecs[:, 0:1], 0.0, ALU.add, ALU.max).then_inc(s_mx, 1)
            dve.wait_ge(s_mx, 1)
            for q in range(4):
                dve.wait_ge(s_abs, 3 + q)
                w = slice(q * 512, (q + 1) * 512)
                v.tensor_tensor(dt[:, w], dt[:, w], sc2[:, w], ALU.add).then_inc(s_dt, 1)
            dve.wait_ge(s_cst, 3)
            for b in range(NSEQ):
                dve.wait_ge(s_dt, b // 2 + 1)
                w = slice(b * L, (b + 1) * L)
                v.tensor_tensor_scan(cum[:, w], ones[:, :], dt[:, w], 0.0, ALU.mult, ALU.add).then_inc(s_cum, 1)
            dve.wait_ge(s_cum, NSEQ)
            v.tensor_scalar(sinT[:, :], cum[:, :], vecs[:, 1:2], float(1 / (2 * np.pi)), ALU.mult, ALU.mult).then_inc(s_tab, 1)
            dve.wait_ge(s_tab, 1)
            v.tensor_scalar(cosT[:, :], sinT[:, :], MAGIC, None, ALU.add).then_inc(s_tab, 1)
            dve.wait_ge(s_tab, 2)
            v.scalar_tensor_tensor(out=sc2[:, :], in0=cosT[:, :], scalar=MAGIC, in1=sinT[:, :],
                                   op0=ALU.subtract, op1=ALU.subtract).then_inc(s_tab, 1)
            for n, dst in enumerate((cumK, dtK, gK)):
                for q in range(4):
                    dve.wait_ge(s_tk, 4 * n + q + 1)
                    v.tensor_copy(dst[:, 4 * q:4 * q + 4, :],
                                  ps[:, q, :].rearrange("p (n h i) -> p n h i", h=H, i=HALF)[:, :, :, 0]).then_inc(s_tkc, 1)
            dve.wait_ge(s_tkc, 12)
            v.tensor_scalar(gK[:, :, :], gK[:, :, :], 1e-30, None, ALU.max).then_inc(s_rat, 1)
            dve.wait_ge(s_rat, 1)
            v.tensor_scalar(gx[:, :, :], gK[:, :, :], 0.25, None, ALU.mult).then_inc(s_rat, 1)
            v.reciprocal(nratio[:, :, :], gK[:, :, :]).then_inc(s_rat, 1)
            dve.wait_ge(s_rat, 3)
            v.tensor_tensor(nratio[:, :, :], nratio[:, :, :], dtK[:, :, :], ALU.mult).then_inc(s_rat, 1)
            dve.wait_ge(s_rat, 4)
            v.tensor_scalar(nratio[:, :, :], nratio[:, :, :], -1.0, 1.0, ALU.mult, ALU.add).then_inc(s_rat, 1)

            def bcast(ap, n):
                return ap.rearrange("p o h -> p h o").broadcast_to([P, H, n])

            def gate(b, j):
                ring = 2 * (b % 2)
                dve.wait_ge(s_th, 2 * b + j + 1)
                if not isinstance(b, int) or b > 1:
                    dve.wait_ge(s_pv, b - 1)
                    dve.wait_ge(s_yg, b - 1)
                v.tensor_tensor(xs[:, bass.ds(ring + j, 1), :].rearrange("p o (h d) -> p (o h) d", h=H),
                                Zb[:, DI:2 * DI].rearrange("p (h d) -> p h d", h=H),
                                bcast(gx[:, bass.ds(2 * b + j, 1), :], HD), ALU.mult).then_inc(s_xs, 1)
                v.scalar_tensor_tensor(out=szr[:, bass.ds(ring + j, 1), :].rearrange("p o d -> p (o d)"),
                                       in0=th[:, j, :], scalar=1.0,
                                       in1=Zb[:, 0:DI], op0=ALU.add, op1=ALU.mult).then_inc(s_sz, 1)

            def turn(b):
                dve.wait_ge(s_bc, b + 1)
                if not isinstance(b, int) or b > 0:
                    dve.wait_ge(s_rope, 2 * b)
                else:
                    dve.wait_ge(s_cos, 1)
                    dve.wait_ge(s_sin, 1)
                for tab, dst in ((cosT, U), (sinT, V)):
                    v.tensor_tensor(dst[:, :, :], BCb, tab[:, bass.ts(b, L)].rearrange("p (o t) -> p o t", o=1)
                                    .broadcast_to([P, 4, L]), ALU.mult).then_inc(s_uv, 1)

            def distances(b):
                dve.wait_ge(s_cb, b + 1)
                if not isinstance(b, int) or b > 0:
                    dve.wait_ge(s_E, 4 * b)
                v.tensor_tensor(D[:, :, 0:2, :].rearrange("p h a t -> p h (a t)"), S0b, bcast(cumK[:, bass.ds(2 * b, 1), :], L),
                                ALU.subtract).then_inc(s_D, 1)
                v.tensor_tensor(D[:, :, 2, :], S0b[:, :, P:L], bcast(cumK[:, bass.ds(2 * b + 1, 1), :], P),
                                ALU.subtract).then_inc(s_D, 1)

            def weigh(b):
                dve.wait_ge(s_S, b + 1)
                dve.wait_ge(s_Em, 2 * b + 2)
                if not isinstance(b, int) or b > 0:
                    dve.wait_ge(s_pv, b)
                v.tensor_tensor(Pm[:, :, 0:2, :].rearrange("p h a t -> p h (a t)"), S0b,
                                E[:, :, 0:2, :].rearrange("p h a t -> p h (a t)"), ALU.mult).then_inc(s_P, 1)
                v.tensor_tensor(Pm[:, :, 2, :], S1b, E[:, :, 2, :], ALU.mult).then_inc(s_P, 1)

            def gated(b):
                dve.wait_ge(s_pv, b + 1)
                dve.wait_ge(s_sz, 2 * b + 2)
                if not isinstance(b, int) or b > 0:
                    dve.wait_ge(s_yT, b)
                    dve.wait_ge(s_ssq, 2 * b)
                v.tensor_tensor(yg[:, :, :], Yb, szr[:, bass.ds(2 * (b % 2), 2), :], ALU.mult).then_inc(s_yg, 1)

            def norm(b):
                dve.wait_ge(s_o, b + 1)
                dve.wait_ge(s_rm, 2 * b + 2)
                for j in range(2):
                    v.scalar_tensor_tensor(out=x1p[:, j, :], in0=Mb[:, j * P:(j + 1) * P], scalar=rms[:, j:j + 1],
                                           in1=hid[:, bass.ds(2 * b + j, 1), :].rearrange("p o d -> p (o d)"),
                                           op0=ALU.mult, op1=ALU.add).then_inc(s_x1p, 1)
                for j in range(2):
                    dve.wait_ge(s_x1p, 2 * b + j + 1)
                    v.bn_stats(st[:, j, :], x1p[:, j, :]).then_inc(s_st, 1)
                for j in range(2):
                    dve.wait_ge(s_rw, 32)
                    dve.wait_ge(s_st, 2 * b + j + 1)
                    v.bn_aggr(mv[:, j, :], st[:, j, :]).then_inc(s_mv, 1)

            def norm_out(b):
                dve.wait_ge(s_rstd, 2 * b + 2)
                if not isinstance(b, int) or b > 0:
                    dve.wait_ge(s_x1T, b)
                for j in range(2):
                    v.tensor_scalar(x1[:, j, :], x1p[:, j, :], mv[:, j, 0:1], rstd[:, j:j + 1],
                                    ALU.subtract, ALU.mult).then_inc(s_x1, 1)

            def keep_logits(b):
                dve.wait_ge(s_lg, b + 1)
                v.tensor_tensor(logits[:, bass.ds(2 * b, 2), :], Mb[:, L:L + 2 * NE].rearrange("p (j e) -> p j e", j=2),
                                rb[:, :].rearrange("p (o e) -> p o e", o=1).broadcast_to([P, 2, NE]),
                                ALU.add).then_inc(s_lgc, 1)

            def step(k):
                if live(k, -2):
                    keep_logits(k - 2)
                if live(k, 0):
                    weigh(k)
                if live(k, 1):
                    turn(k + 1)
                    distances(k + 1)
                if live(k, -1):
                    norm(k - 1)
                if live(k, 1):
                    gate(k + 1, 0)
                if live(k, 0):
                    gated(k)
                if live(k, 1):
                    gate(k + 1, 1)
                if live(k, -1):
                    norm_out(k - 1)

            dve.wait_ge(s_rw, 32)
            steps(dve, step)

            def split_low(e, slot):
                dve.wait_ge(s_wh, 2 * e + 2)
                if not isinstance(e, int) or e > 1:
                    dve.wait_ge(s_O, 4 * e - 4)
                for lo, hi, raw in ((w1l, w1h, w1r), (w2l, w2h, w2r)):
                    v.scalar_tensor_tensor(out=lo[:, slot, :], in0=raw[:, slot, 0:FF], scalar=WS, in1=hi[:, slot, :],
                                           op0=ALU.mult, op1=ALU.subtract).then_inc(s_wl, 1)
                v.tensor_copy(b1s[:, slot, :], w1r[:, slot, FF:FF + FC]).then_inc(s_wl, 1)
                v.tensor_scalar(b2s[:, slot:slot + 1], w1r[:, slot, FF + FC:FF + FC + 1], WS, None, ALU.mult).then_inc(s_wl, 1)

            split_low(0, 0)
            split_low(1, 1)

            n = [0]

            def did(ins):
                n[0] += 1
                ins.then_inc(s_rt, 1)

            def rowb(i):
                return rs[:, i, :].rearrange("p (n o) -> p n o", o=1).broadcast_to([P, NT, NE])

            dve.wait_ge(s_lgc, NSEQ)
            dve.wait_ge(s_cst, 8)
            v.tensor_reduce(rs[:, 0, :], logits[:, :, :], AX_X, ALU.max).then_inc(s_rt, 1)
            dve.wait_ge(s_rt, 1)
            v.tensor_tensor(rt[:, 1, :, :], logits[:, :, :], rowb(0), ALU.subtract).then_inc(s_rt, 1)
            dve.wait_ge(s_rt, 2)
            v.tensor_scalar(rt[:, 3, :, :], iota8[:, :, :], float(NE), None, ALU.subtract).then_inc(s_rt, 1)
            v.tensor_scalar(rt[:, 4, :, :], rt[:, 1, :, :], 0.0, None, ALU.is_equal).then_inc(s_rt, 1)
            dve.wait_ge(s_rt, 4)
            v.tensor_tensor(rt[:, 5, :, :], rt[:, 4, :, :], rt[:, 3, :, :], ALU.mult).then_inc(s_rt, 1)
            dve.wait_ge(s_rt, 5)
            v.tensor_reduce(rs[:, 1, :], rt[:, 5, :, :], AX_X, ALU.min).then_inc(s_rt, 1)
            dve.wait_ge(s_rt, 6)
            v.tensor_tensor(rt[:, 4, :, :], rt[:, 3, :, :], rowb(1), ALU.is_equal).then_inc(s_rt, 1)
            dve.wait_ge(s_rt, 7)
            v.scalar_tensor_tensor(out=rt[:, 5, :, :], in0=rt[:, 4, :, :], scalar=-3e38, in1=rt[:, 1, :, :],
                                   op0=ALU.mult, op1=ALU.add).then_inc(s_rt, 1)
            dve.wait_ge(s_rt, 8)
            v.tensor_reduce(rs[:, 2, :], rt[:, 5, :, :], AX_X, ALU.max).then_inc(s_rt, 1)
            dve.wait_ge(s_rt, 9)
            v.tensor_tensor(rt[:, 6, :, :], rt[:, 5, :, :], rowb(2), ALU.is_equal).then_inc(s_rt, 1)
            dve.wait_ge(s_rt, 10)
            v.tensor_tensor(rt[:, 6, :, :], rt[:, 6, :, :], rt[:, 3, :, :], ALU.mult).then_inc(s_rt, 1)
            dve.wait_ge(s_rt, 11)
            v.tensor_reduce(rs[:, 3, :], rt[:, 6, :, :], AX_X, ALU.min).then_inc(s_rt, 1)
            dve.wait_ge(s_rt, 12)
            v.tensor_tensor(rt[:, 6, :, :], rt[:, 3, :, :], rowb(3), ALU.is_equal).then_inc(s_rt, 1)
            dve.wait_ge(s_rt, 13)
            v.tensor_tensor(rt[:, 4, :, :], rt[:, 4, :, :], rt[:, 6, :, :], ALU.add).then_inc(s_rt, 1)
            dve.wait_ge(s_rte, 1)
            v.tensor_reduce(rs[:, 4, :], rt[:, 2, :, :], AX_X, ALU.add).then_inc(s_rt, 1)
            dve.wait_ge(s_rt, 15)
            v.reciprocal(rs[:, 5, :], rs[:, 4, :]).then_inc(s_rt, 1)
            v.tensor_tensor(rt[:, 4, :, :], rt[:, 4, :, :], rt[:, 2, :, :], ALU.mult).then_inc(s_rt, 1)
            dve.wait_ge(s_rt, 17)
            v.tensor_tensor(rt[:, 4, :, :], rt[:, 4, :, :], rowb(5), ALU.mult).then_inc(s_rt, 1)
            dve.wait_ge(s_rt, 18)
            v.tensor_reduce(rs[:, 6, :], rt[:, 4, :, :], AX_X, ALU.add).then_inc(s_rt, 1)
            dve.wait_ge(s_rt, 19)
            v.tensor_scalar(rs[:, 6, :], rs[:, 6, :], 1e-9, None, ALU.add).then_inc(s_rt, 1)
            dve.wait_ge(s_rt, 20)
            v.reciprocal(rs[:, 7, :], rs[:, 6, :]).then_inc(s_rt, 1)
            dve.wait_ge(s_rt, 21)
            v.tensor_tensor(rt[:, 7, :, :], rt[:, 4, :, :], rowb(7), ALU.mult).then_inc(s_rt, 1)
            dve.wait_ge(s_cT, 1)
            v.tensor_scalar(combT[:, :], ps[:, 6, 0:P], 1.0 / WS, None, ALU.mult).then_inc(s_cTc, 1)

            def low(u, par, first=False):
                for q in range(2):
                    if not first and q == 0:
                        dve.wait_ge(s_O, u - 1)
                    dve.wait_ge(s_gh, 2 * u + q + 1)
                    w = slice(2 * q * CH, 2 * (q + 1) * CH)
                    v.tensor_tensor(gl[:, par, w], g[par][:, w], gh[:, par, w], ALU.subtract).then_inc(s_gl, 1)

            def add_unit(u, e, slot, c, count=None):
                w = slice(c * CH, (c + 1) * CH)
                if c == 0:
                    dve.wait_ge(s_cbc[slot], count)
                    dve.wait_ge(s_wl, 4 * e + 4)
                dve.wait_ge(s_O, u + 1)
                v.scalar_tensor_tensor(out=tmp[:, c % 2, :], in0=ps[:, 4 + c % 2, :], scalar=b2s[:, slot:slot + 1],
                                       in1=cbc[slot][:, w], op0=ALU.add, op1=ALU.mult).then_inc(s_ob, 1)
                dve.wait_ge(s_ob, u + 3)
                v.tensor_tensor(acc[:, w], acc[:, w], tmp[:, c % 2, :], ALU.add).then_inc(s_acc, 1)

            v.memset(tmp[:, :, :], 0.0).then_inc(s_ob, 2)
            dve.wait_ge(s_ob, 2)
            dve.wait_ge(s_x1a, NSEQ)
            low(0, 0, first=True)
            low(1, 1, first=True)
            for j in range(8):
                if j == 4:
                    split_low(2, 0)
                add_unit(j, j // 4, j // 4, j % 4, 16)
                low(j + 2, j % 2)
            with dve.Fori(1, NE // 2) as k:
                for j in range(8):
                    if j % 4 == 0:
                        split_low(2 * k + 1 + j // 4, 1 - j // 4)
                    add_unit(8 * k + j, 2 * k + j // 4, j // 4, j % 4, 16 * k + 16)
                    low(8 * k + j + 2, j % 2)

            def finish(c):
                for q in range(4):
                    dve.wait_ge(s_ft, c + 1)
                    v.bn_stats(fst[:, q, :], ps[:, 6 + c % 2, q * P:(q + 1) * P]).then_inc(s_fst, 1)
                for q in range(4):
                    dve.wait_ge(s_fst, 4 * c + q + 1)
                    v.bn_aggr(fmv[:, q, :], fst[:, q, :]).then_inc(s_fmv, 1)
                dve.wait_ge(s_frs, 2 * c + 2)
                for q in range(4):
                    v.tensor_scalar(outb[:, 4 * c + q, :], ps[:, 6 + c % 2, q * P:(q + 1) * P], fmv[:, q, 0:1],
                                    frs[:, q:q + 1], ALU.subtract, ALU.mult).then_inc(s_fin, 1)

            dve.wait_ge(s_wl, 4 * NE + 4)
            dve.wait_ge(s_acc, 4 * NE)
            v.tensor_scalar(acc[:, :], acc[:, :], w1r[:, 0, FF + FC:FF + FC + 1], None, ALU.add).then_inc(s_acc, 1)
            for c in range(NCH):
                w = slice(c * CH, (c + 1) * CH)
                u = 4 * NE + c
                dve.wait_ge(s_O, u + 1)
                dve.wait_ge(s_acc, 4 * NE + 1)
                v.scalar_tensor_tensor(out=acc[:, w], in0=ps[:, 4 + c % 2, :], scalar=1.0 / WS,
                                       in1=acc[:, w], op0=ALU.mult, op1=ALU.add).then_inc(s_acc, 1)
                if c + 2 < NCH:
                    low(u + 2, c % 2)
                if c > 0:
                    finish(c - 1)
            finish(NCH - 1)

        @block.tensor
        def _(pe):
            te = nc.tensor
            pe.wait_ge(s_id, 1)
            for q in range(4):
                pe.wait_ge(s_hid[q], 16)
                for j in range(4):
                    m = te.transpose(ps[:, q, j * P:(j + 1) * P], hid[:, 4 * q + j, :], ident[:, :])
                m.then_inc(s_hT, 1)
            pe.wait_ge(s_w, 32)
            for q in range(4):
                pe.wait_ge(s_hTc, q + 1)
                te.matmul(ps[:, 4 + q, :], wdt[:, :], hidT[:, 512 * q:512 * q + 512], start=True,
                          stop=True).then_inc(s_dtp, 1)
            for n, src in enumerate((cum, dt, sc1)):
                if n == 0:
                    pe.wait_ge(s_cum, NSEQ)
                if n == 2:
                    pe.wait_ge(s_gs, 2)
                for q in range(4):
                    if n > 0:
                        pe.wait_ge(s_tkc, 4 * (n - 1) + q + 1)
                    for j in range(4):
                        t0 = (4 * q + j) * P
                        m = te.transpose(ps[:, q, j * P:(j + 1) * P], src[:, t0:t0 + P], ident[:, :])
                    m.then_inc(s_tk, 1)

            def spread(b):
                if not isinstance(b, int) or b > 0:
                    pe.wait_ge(s_P, 2 * b)
                for h in range(H):
                    m = te.matmul(S0b[:, h, :], sel[:, h, :], cum[:, bass.ts(b, L)], start=True, stop=True)
                m.then_inc(s_cb, 1)

            def scores(b):
                pe.wait_ge(s_bm, 4 * b + 4)
                pe.wait_ge(s_rope, 2 * b + 2)
                pe.wait_ge(s_D, 2 * b + 2)
                for h in range(H):
                    for e in range(2):
                        te.matmul(S0b[:, h, :], Bm[:, h, e, 0:P], R[:, 2 + e, :], start=(e == 0), stop=(e == 1))
                for h in range(H):
                    for e in range(2):
                        m = te.matmul(S1b[:, h, :], Bm[:, h, e, P:L], R[:, 2 + e, P:L], start=(e == 0), stop=(e == 1))
                m.then_inc(s_S, 1)

            def project_zx(b, j):
                if j == 0:
                    pe.wait_ge(s_hTb, b + 1)
                if not isinstance(b, int) or b > 0 or j > 0:
                    pe.wait_ge(s_sz, 2 * b + j)
                te.matmul(Zb, hTb[:, j * P:(j + 1) * P], win[:, Z0:B0], start=True, stop=True).then_inc(s_zx, 1)

            def project_bc(b):
                pe.wait_ge(s_hTb, b + 1)
                if not isinstance(b, int) or b > 0:
                    pe.wait_ge(s_uv, 2 * b)
                for n, c0 in enumerate((B0, B0 + 1, C0, C0 + 1)):
                    m = te.matmul(BCb[:, n, :], win[:, c0:c0 + DI - 1:2], hTb[:, :], start=True, stop=True)
                m.then_inc(s_bc, 1)

            def values(b):
                pe.wait_ge(s_P, 2 * b + 2)
                pe.wait_ge(s_xs, 2 * b + 2)
                if not isinstance(b, int) or b > 0:
                    pe.wait_ge(s_yg, b)
                ring = 2 * (b % 2)
                for h in range(H):
                    f = slice(h * HD, (h + 1) * HD)
                    x0 = xs[:, bass.ds(ring, 1), f].rearrange("p o d -> p (o d)")
                    x1_ = xs[:, bass.ds(ring + 1, 1), f].rearrange("p o d -> p (o d)")
                    te.matmul(Yb[:, 0, f], Pm[:, h, 0, :], x0, start=True, stop=True)
                    te.matmul(Yb[:, 1, f], Pm[:, h, 1, :], x0, start=True, stop=False)
                    m = te.matmul(Yb[:, 1, f], Pm[:, h, 2, :], x1_, start=False, stop=True)
                m.then_inc(s_pv, 1)

            def turn_y(b):
                pe.wait_ge(s_yg, b + 1)
                if not isinstance(b, int) or b > 0:
                    pe.wait_ge(s_lgc, b)
                for j in range(2):
                    for c in range(2):
                        n = 2 * j + c
                        m = te.transpose(Mb[:, n * P:(n + 1) * P], yg[:, j, c * P:(c + 1) * P], ident[:, :])
                m.then_inc(s_yT, 1)

            def project_out(b):
                pe.wait_ge(s_yTc, b + 1)
                if isinstance(b, int) and b == 0:
                    pe.wait_ge(s_wo, 2)
                for j in range(2):
                    for c in range(2):
                        m = te.matmul(Mb[:, j * P:(j + 1) * P], yT[:, j, c, :], wout[:, c, :], start=(c == 0), stop=(c == 1))
                m.then_inc(s_o, 1)

            def turn_x1(b):
                pe.wait_ge(s_x1, 2 * b + 2)
                for j in range(2):
                    m = te.transpose(Mb[:, j * P:(j + 1) * P], x1[:, j, :], ident[:, :])
                m.then_inc(s_x1T, 1)

            def route(b):
                pe.wait_ge(s_x1Tb, b + 1)
                for j in range(2):
                    m = te.matmul(Mb[:, L + j * NE:L + (j + 1) * NE], x1Tb[:, j * P:(j + 1) * P], rw[:, :], start=True, stop=True)
                m.then_inc(s_lg, 1)

            def step(k):
                if live(k, -2):
                    route(k - 2)
                if live(k, 0):
                    scores(k)
                if live(k, -1):
                    turn_y(k - 1)
                if live(k, 1):
                    project_bc(k + 1)
                    spread(k + 1)
                if live(k, -1):
                    project_out(k - 1)
                if live(k, 1):
                    project_zx(k + 1, 0)
                if live(k, 0):
                    values(k)
                if live(k, 1):
                    project_zx(k + 1, 1)
                if live(k, -1):
                    turn_x1(k - 1)

            pe.wait_ge(s_id, 2)
            pe.wait_ge(s_rw, 32)
            pe.wait_ge(s_tkc, 12)
            pe.wait_ge(s_mx, 1)
            steps(pe, step)

            def product(bank, ah, al, bh, bl, start, stop):
                te.matmul(bank, ah, bh, start=start, stop=False)
                te.matmul(bank, ah, bl, start=False, stop=False)
                return te.matmul(bank, al, bh, start=False, stop=stop)

            def first(u, e, slot, c, start=False):
                if c == 0:
                    pe.wait_ge(s_wl, 4 * e + 4)
                w = slice(c * CH, (c + 1) * CH)
                for f in range(FC):
                    if not start:
                        pe.wait_ge(s_g, 4 * u + f - 3)
                    fs = slice(f * P, (f + 1) * P)
                    product(ps[:, f, :], w1h[:, slot, fs], w1l[:, slot, fs], x1h[:, w], x1l[:, w],
                            True, True).then_inc(s_h, 1)

            def second(u, slot, par):
                for f in range(FC):
                    if f % 2 == 0:
                        pe.wait_ge(s_gl, 2 * u + f // 2 + 1)
                    fs, gs = slice(f * P, (f + 1) * P), slice(f * CH, (f + 1) * CH)
                    m = product(ps[:, 4 + par, :], w2h[:, slot, fs], w2l[:, slot, fs], gh[:, par, gs], gl[:, par, gs],
                                f == 0, f == FC - 1)
                m.then_inc(s_O, 1)

            pe.wait_ge(s_x1l, NSEQ)
            first(0, 0, 0, 0, start=True)
            first(1, 0, 0, 1)
            pe.wait_ge(s_rt, 22)
            te.transpose(ps[:, 6, 0:P], rt[:, 7, :, :].rearrange("p n e -> p (n e)"), ident[:, :]).then_inc(s_cT, 1)
            with pe.Fori(0, NE // 2) as k:
                for j in range(8):
                    n = j + 2
                    first(8 * k + n, 2 * k + n // 4, n // 4 % 2, n % 4)
                    pe.wait_ge(s_ob, 8 * k + j + 1)
                    second(8 * k + j, j // 4, j % 2)

            def turn_out(c):
                pe.wait_ge(s_acc, 4 * NE + c + 2)
                if c >= 2:
                    pe.wait_ge(s_fin, 4 * (c - 1))
                for q in range(4):
                    t0 = c * CH + q * P
                    m = te.transpose(ps[:, 6 + c % 2, q * P:(q + 1) * P], acc[:, t0:t0 + P], ident[:, :])
                m.then_inc(s_ft, 1)

            for c in range(NCH):
                if c + 2 < NCH:
                    first(4 * NE + c + 2, NE, 0, c + 2)
                if c < 2:
                    pe.wait_ge(s_ob, 4 * NE + c + 1)
                else:
                    pe.wait_ge(s_acc, 4 * NE + c)
                second(4 * NE + c, 0, c % 2)
                if c > 0:
                    turn_out(c - 1)
            turn_out(NCH - 1)


def live(k, off):
    return not isinstance(k, int) or 0 <= k + off < NSEQ


def steps(engine, step):
    for k in (-1, 0, 1):
        step(k)
    with engine.Fori(2, NSEQ - 1) as k:
        step(k)
    for k in (NSEQ - 1, NSEQ, NSEQ + 1):
        step(k)


def kernel(**inputs):
    import concourse.bacc as _bacc
    from concourse.bass_utils import run_bass_kernel_spmd as _run

    a = {k: np.asarray(v) for k, v in inputs.items()}
    at, ff = "L0_attn_", "L0_ffn_"
    w_in = a[at + "W_in"]
    half = np.arange(HALF, dtype=np.float32) / np.float32(HALF)
    inv = (np.float32(1.0) / np.power(np.float32(10000.0), half)).astype(np.float32)
    arrays = {
        "hidden": a[at + "hidden"].reshape(T, P),
        "w_in": w_in,
        "w_dt": np.repeat(w_in[:, DT0:DT0 + H], HALF, axis=1),
        "dt_bias": np.repeat(a[at + "dt_bias"], HALF).reshape(P, 1),
        "a_log": np.broadcast_to(a[at + "A_log"][None, :], (P, H)),
        "norm_w": a[at + "norm_weight"].reshape(2, P).T,
        "w_out": a[at + "W_out"],
        "inv_freq": np.tile(inv, H).reshape(P, 1),
        "w1": np.concatenate([
            np.concatenate([a[ff + "exp_w1"], a[ff + "shared_w1"][None]], axis=0),
            np.concatenate([a[ff + "exp_b1"], a[ff + "shared_b1"][None]], axis=0).reshape(NE + 1, FC, P).transpose(0, 2, 1),
            np.concatenate([a[ff + "exp_b2"], a[ff + "shared_b2"][None]], axis=0)[:, :, None]], axis=2),
        "w2": np.concatenate([a[ff + "exp_w2"], a[ff + "shared_w2"][None]], axis=0),
        "router_w": a[ff + "router_w"],
        "router_b": np.broadcast_to(a[ff + "router_b"][None, :], (P, NE)),
    }
    nc = _bacc.Bacc("TRN2", target_bir_lowering=False, num_devices=1)
    feed, args = {}, []
    for name, x in arrays.items():
        x = np.ascontiguousarray(x)
        feed[f"in_{name}"] = x
        args.append(nc.dram_tensor(f"in_{name}", x.shape, mybir.dt.from_np(x.dtype), kind="ExternalInput").ap())
    comb = nc.dram_tensor("comb_dram", (NT * NE, P), F32, kind="Internal").ap()
    out = nc.dram_tensor("out_0", (T, P), F32, kind="ExternalOutput").ap()
    build(nc, *args, comb, out)
    r = _run(nc, [feed], core_ids=[0])
    return r.results[0]["out_0"].reshape(NSEQ, L, P)
```

```python
from contextlib import ExitStack

import numpy as np

import concourse.bass as bass
from concourse import mybir

ALU = mybir.AluOpType
ACT = mybir.ActivationFunctionType
F32 = mybir.dt.float32
F16 = mybir.dt.float16
I32 = mybir.dt.int32
U32 = mybir.dt.uint32
AX_X = mybir.AxisListType.X

P = 128
NSEQ, L = 8, 256
T = NSEQ * L
NT = T // P
H, HD = 4, 64
HALF = 32
DI = H * HD
FF, NE = 512, 8
FC = FF // P
TS = 256
NR = 2 * T // TS + NE - 1
NS0 = 4
NU = NR + T // TS
LOOP0, LOOP1 = NS0 + 2, NS0 + (NR - 3) // 2 * 2
EARLY = 1
NSEL, NPOS = 15, 7
RW = P + 4
NROW = NE * T + TS
FILL = 10
CH = 512
NCH = T // CH
Z0, X0, B0, C0, DT0 = 0, DI, 2 * DI, 3 * DI, 4 * DI
RMS_EPS, LN_EPS = 1e-6, 1e-5
MAGIC = 12582912.0
TURN = 6.283185005187988
WS = 256.0
FAR = 1e30


def build(nc, hidden, w_in, w_dt, vectors, w_out, w1, w2, b1, b2, xg, yk, out):
    ctx = ExitStack()
    with ctx:
        def sb(name, shape, dt=F32):
            return ctx.enter_context(nc.sbuf_tensor(name, shape, dt))

        def sem(name):
            return ctx.enter_context(nc.semaphore(name))

        hid = sb("hid", [P, NT, RW])
        rows = sb("rows", [P, 4, 2, 2, RW])
        hidT = sb("hidT", [P, T])
        win = sb("win", [P, 4 * DI + H])
        wdt = sb("wdt", [P, P])
        wout = sb("wout", [P, 2, P])
        vecs = sb("vecs", [P, 32])
        half = sb("half", [P, 4])
        epsr = sb("epsr", [P, 2])
        epsl = sb("epsl", [P, 4])
        rw = vecs[:, 8:8 + NE]
        rb = vecs[:, 8 + NE:8 + 2 * NE]
        expA = sb("expA", [P, H])
        half_pi = sb("half_pi", [P, 1])
        ident = sb("ident", [P, P])
        sel = sb("sel", [P, H, P])
        ones = sb("ones", [P, L])
        dt = sb("dt", [P, T])
        cum = sb("cum", [P, T])
        cosT = sb("cosT", [P, T])
        sinT = sb("sinT", [P, T])
        sc1 = sb("sc1", [P, T])
        sc2 = sb("sc2", [P, T])
        cumK = sb("cumK", [P, NT, H])
        dtK = sb("dtK", [P, NT, H])
        gK = sb("gK", [P, NT, H])
        gx = sb("gx", [P, NT, H])
        nratio = sb("nratio", [P, NT, H])
        hTb = sb("hTb", [P, L])
        th = sb("th", [P, 2, DI])
        szr = sb("szr", [P, 4, DI])
        xs = sb("xs", [P, 4, DI])
        U = sb("U", [P, 4, L])
        V = sb("V", [P, 4, L])
        R = sb("R", [P, 4, L])
        Bm = sb("Bm", [P, H, 2, L])
        D = sb("D", [P, H, 3, P])
        E = sb("E", [P, H, 3, P])
        DI0 = sb("DI0", [P, 2, H, P])
        Pm = sb("Pm", [P, H, 3, P])
        yg = sb("yg", [P, 2, DI])
        sq = sb("sq", [P, DI])
        ssq = sb("ssq", [P, 2])
        rms = sb("rms", [P, 2])
        yT = sb("yT", [P, 2, 2, P])
        x1p = sb("x1p", [P, 2, P])
        st = sb("st", [P, 2, 6])
        mv = sb("mv", [P, 2, 2])
        rstd = sb("rstd", [P, 2])
        x1 = sb("x1", [P, 2, P])
        x1Tb = sb("x1Tb", [P, L])
        x1h = sb("x1h", [P, T], F16)
        x1l = sb("x1l", [P, T], F16)
        LR = sb("LR", [P, 6 * NE])
        lg = sb("lg", [P, 2, NE])
        dS = sb("dS", [P, 2, NE])
        d2 = sb("d2", [P, 2, NE])
        q1 = sb("q1", [P, 2, NE])
        q2 = sb("q2", [P, 2, NE])
        q3 = sb("q3", [P, 2, NE])
        o12 = sb("o12", [P, 2, 2, NE])
        chosen = sb("chosen", [P, 2, NE])
        rr = sb("rr", [P, 4, 2])
        im8 = sb("im8", [P, 2, NE])
        below = sb("below", [P, P])
        cnt = sb("cnt", [P, 2, NE])
        part0 = sb("part0", [P, NE])
        pos = sb("pos", [P, 2, NE])
        pq = sb("pq", [P, 2, 2, NE])
        pf = sb("pf", [P, 4])
        posu = sb("posu", [P, 4, 4], U32)
        dall = sb("dall", [P, NT, NE])
        r2all = sb("r2all", [P, NT])
        ex = sb("ex", [P, NT, NE])
        wk = sb("wk", [P, 8, NT])
        tb = sb("tb", [P, 6, NE])
        tg = sb("tg", [P, NR + 1, NE])
        tg2 = sb("tg2", [P, NR + 1, NE])
        tr = sb("tr", [P, 6, NR + 1])
        iotaR = sb("iotaR", [P, NR + 1, NE])
        tabs = sb("tabs", [P, 2, NR + 1], I32)
        w1r = sb("w1r", [P, 2, FF])
        w2r = sb("w2r", [P, 2, FC * P])
        b1a = sb("b1a", [P, NE + 1, FC])
        bcur = sb("bcur", [P, 2, FC])
        b2a = sb("b2a", [1, NE + 1, P])
        b2p = sb("b2p", [1, NE + 1, 2, P], F16)
        one16 = sb("one16", [1, P], F16)
        w2p = sb("w2p", [P, NE + 1, FC, 2, P], F16)
        ws1 = sb("ws1", [P, 2, FF], F16)
        xh = sb("xh", [P, 2, TS], F16)
        xl = sb("xl", [P, 2, TS], F16)
        idall = sb("idall", [P, NR, 2], U32)
        idc = sb("idc", [P, 2, 2], U32)
        fst = sb("fst", [P, NT, 6])
        fmv = sb("fmv", [P, NT, 2])
        frs = sb("frs", [P, NT])
        fnm = sb("fnm", [P, NT])
        carry = sb("carry", [P, 2])
        wy1 = sb("wy1", [P, 2, 4, P])
        wy2 = sb("wy2", [P, 2, 4, P])
        w1h = sc1[:, :].bitcast(F16).rearrange("p (e f) -> p e f", f=FF)
        w1l = sc2[:, :].bitcast(F16).rearrange("p (e f) -> p e f", f=FF)
        g = dt[:, :].rearrange("p (r f) -> p r f", r=2)
        gh = U[:, :, :].rearrange("p a b -> p (a b)").bitcast(F16).rearrange("p (r f) -> p r f", r=2)
        gl = V[:, :, :].rearrange("p a b -> p (a b)").bitcast(F16).rearrange("p (r f) -> p r f", r=2)
        xt = cum[:, 0:4 * RW].rearrange("p (r s f) -> p r s f", r=2, s=2)
        yr = cum[:, 4 * RW:4 * RW + 512].rearrange("p (r s f) -> p r s f", r=2, s=2)
        tmp = cum[:, 4 * RW + 512:4 * RW + 1024].rearrange("p (r s f) -> p r s f", r=2, s=2)
        acc = hidT[:, :].rearrange("p (n f) -> p n f", f=P)
        ytk = [tab[:, q * 1024:(q + 1) * 1024].rearrange("p (n c f) -> p n c f", n=4, c=2)
               for tab in (cosT, sinT) for q in range(2)]
        filler = Pm[:, :, :, :].rearrange("p a b c -> p (a b c)")[:, 0:FILL * RW].rearrange("p (n f) -> p n f", f=RW)

        ps = ctx.enter_context(nc.psum_tensor("ps", [P, 8, 512], F32))
        Zb = ps[:, 0, :]
        BCb = ps[:, 1:3, :].rearrange("p a b -> p (a b)").rearrange("p (f t) -> p f t", t=L)
        S0b = ps[:, 3:5, :].rearrange("p a b -> p (a b)").rearrange("p (h t) -> p h t", t=L)
        S1b = ps[:, 5, :].rearrange("p (h t) -> p h t", t=P)
        Yb = ps[:, 6, :].rearrange("p (j f) -> p j f", j=2)
        Mb = ps[:, 7, :]
        Ob = [ps[:, 4 + q, :].rearrange("p (s l d) -> p s l d", s=2, l=2) for q in range(2)]
        dtb = ps[:, 4:8, :].rearrange("p a b -> p (a b)")

        s_hid = [sem(f"s_hid{q}") for q in range(4)]
        s_w = sem("s_w")
        s_wdt = sem("s_wdt")
        s_vec = sem("s_vec")
        s_rw = sem("s_rw")
        s_cst = sem("s_cst")
        s_id = sem("s_id")
        s_hT = sem("s_hT")
        s_hTc = sem("s_hTc")
        s_dtp = sem("s_dtp")
        s_abs = sem("s_abs")
        s_A = sem("s_A")
        s_Aneg = sem("s_Aneg")
        s_wo = sem("s_wo")
        s_mx = sem("s_mx")
        s_dt = sem("s_dt")
        s_gs = sem("s_gs")
        s_cum = sem("s_cum")
        s_tab = sem("s_tab")
        s_absr = sem("s_absr")
        s_cos = sem("s_cos")
        s_sin = sem("s_sin")
        s_tk = sem("s_tk")
        s_tkc = sem("s_tkc")
        s_rat = sem("s_rat")
        s_hTb = sem("s_hTb")
        s_zx = sem("s_zx")
        s_th = sem("s_th")
        s_xs = sem("s_xs")
        s_sz = sem("s_sz")
        s_bc = sem("s_bc")
        s_uv = sem("s_uv")
        s_rope = sem("s_rope")
        s_bm = sem("s_bm")
        s_cb = sem("s_cb")
        s_D = sem("s_D")
        s_Dm = sem("s_Dm")
        s_di = sem("s_di")
        s_E = sem("s_E")
        s_Em = sem("s_Em")
        s_S = sem("s_S")
        s_P = sem("s_P")
        s_pv = sem("s_pv")
        s_yg = sem("s_yg")
        s_ssq = sem("s_ssq")
        s_rm = sem("s_rm")
        s_yT = sem("s_yT")
        s_yTc = sem("s_yTc")
        s_o = sem("s_o")
        s_x1p = sem("s_x1p")
        s_st = sem("s_st")
        s_mv = sem("s_mv")
        s_rstd = sem("s_rstd")
        s_x1 = sem("s_x1")
        s_x1T = sem("s_x1T")
        s_x1Tb = sem("s_x1Tb")
        s_x1h = sem("s_x1h")
        s_x1l = sem("s_x1l")
        s_lg = sem("s_lg")
        s_lgc = sem("s_lgc")
        s_b2 = sem("s_b2")
        s_fr = sem("s_fr")
        s_fill = sem("s_fill")
        s_xrow = sem("s_xrow")
        s_rows = sem("s_rows")
        s_row1 = sem("s_row1")
        s_sel = sem("s_sel")
        s_rk = sem("s_rk")
        s_rkc = sem("s_rkc")
        s_pos = sem("s_pos")
        s_xg = sem("s_xg")
        s_tb = sem("s_tb")
        s_ex = sem("s_ex")
        s_wk = sem("s_wk")
        s_we = sem("s_we")
        s_wh = sem("s_wh")
        s_wl = sem("s_wl")
        s_xt = [sem(f"s_xt{q}") for q in range(2)]
        s_turn = sem("s_turn")
        s_bc1 = sem("s_bc1")
        s_xh = sem("s_xh")
        s_xl = sem("s_xl")
        s_ida = sem("s_ida")
        s_h = sem("s_h")
        s_g = sem("s_g")
        s_gh = sem("s_gh")
        s_gl = sem("s_gl")
        s_O = sem("s_O")
        s_ob = sem("s_ob")
        s_id2 = sem("s_id2")
        s_y = sem("s_y")
        s_yk = [sem(f"s_yk{q}") for q in range(2)]
        s_ax = sem("s_ax")
        s_carry = sem("s_carry")
        s_ytk = [sem(f"s_ytk{q}") for q in range(NCH)]
        s_wy1 = sem("s_wy1")
        s_wy2 = sem("s_wy2")
        s_c = sem("s_c")
        s_fst = sem("s_fst")
        s_fmv = sem("s_fmv")
        s_frs = sem("s_frs")
        s_fnm = sem("s_fnm")
        s_fin = sem("s_fin")
        s_out = sem("s_out")

        block = ctx.enter_context(nc.Block())

        NVEC = 8

        @block.sync
        def _(sp):
            hv = hidden.rearrange("(n p) d -> p n d", p=P)
            for q in range(4):
                sp.dma_start(hid[:, 4 * q:4 * q + 4, 0:P], hv[:, 4 * q:4 * q + 4, :]).then_inc(s_hid[q], 16)

            def load_expert(e):
                if not isinstance(e, int) or e > 0:
                    sp.wait_ge(s_we, 32 * e)
                if not isinstance(e, int) or e > 1:
                    sp.wait_ge(s_wl, 2 * e - 2)
                slot = bass.ds(e % 2, 1)
                src1 = w1[bass.ds(e, 1)].rearrange("o p f -> p (o f)")
                src2 = w2[bass.ds(e, 1)].rearrange("o (c p) d -> p (o c) d", p=P)
                sp.dma_start(w1r[:, slot, :].rearrange("p o f -> p (o f)"), src1).then_inc(s_we, 16)
                sp.dma_start(w2r[:, slot, :].rearrange("p o (c d) -> p (o c) d", c=FC), src2).then_inc(s_we, 16)

            sp.wait_ge(s_fr, 2)
            xf = xg.rearrange("(q p n) f -> q p n f", p=P, n=FILL)
            for q in range(NROW // (P * FILL)):
                sp.dma_start(xf[q], filler).then_inc(s_fill, 16)
            load_expert(0)
            load_expert(1)
            with sp.Fori(2, NE + 1) as e:
                load_expert(e)

            def load_rows(r, par):
                row = sp.value_load(tabs[0:1, 1, bass.ds(r, 1)], min_val=0, max_val=NROW - TS)
                sp.dma_start(xt[:, par, :, :], xg[bass.ds(row, TS), :].rearrange("(p s) f -> p s f", s=2)).then_inc(s_xt[par], 16)

            sp.wait_ge(s_tb, 13)
            sp.wait_ge(s_xg, 64 * NSEQ)
            load_rows(0, 0)
            load_rows(1, 1)

            def reload_rows(r, par):
                sp.wait_ge(s_ida, r - 1)
                sp.wait_ge(s_turn, r - 1)
                load_rows(r, par)

            with sp.Fori(1, NR // 2) as k:
                reload_rows(2 * k, 0)
                reload_rows(2 * k + 1, 1)
            reload_rows(NR - 1, (NR - 1) % 2)
            ykv = yk.rearrange("(n p c) f -> p n c f", p=P, c=2)
            sp.wait_ge(s_yk[0], 32 * ((NR + 1) // 2))
            sp.wait_ge(s_yk[1], 32 * (NR // 2))
            for c in range(NCH):
                sp.dma_start(ytk[c], ykv[:, 4 * c:4 * c + 4]).then_inc(s_ytk[c], 16)
            ov = out.rearrange("(n p) d -> p n d", p=P)
            for c in range(NCH):
                sp.wait_ge(s_fin, 4 * (c + 1))
                sp.dma_start(ov[:, 4 * c:4 * c + 4, :], acc[:, 4 * c:4 * c + 4, :]).then_inc(s_out, 16)
            sp.wait_ge(s_out, 16 * NCH)

        @block.gpsimd
        def _(pool):
            gp = nc.gpsimd
            gp.memset(filler, 0.0).then_inc(s_fr, 1)
            pool.wait_ge(s_fr, 1)
            gp.memset(filler[:, :, P:RW], float(2 * T)).then_inc(s_fr, 1)
            gp.memset(ident[:, :], 0.0).then_inc(s_cst, 1)
            gp.memset(sel[:, :, :], 0.0).then_inc(s_cst, 1)
            pool.wait_ge(s_cst, 2)
            gp.affine_select(out=ident[:, :], in_=ident[:, :], compare_op=ALU.not_equal, fill=1.0,
                             base=0, pattern=[[-1, P]], channel_multiplier=1).then_inc(s_id, 1)
            gp.affine_select(out=sel[:, :, :], in_=sel[:, :, :], compare_op=ALU.not_equal, fill=1.0,
                             base=0, pattern=[[-HALF, H], [0, P]], channel_multiplier=1).then_inc(s_id, 1)
            gp.memset(ones[:, :], 1.0).then_inc(s_cst, 1)
            gp.memset(half[:, :], -0.5).then_inc(s_cst, 1)
            gp.memset(epsr[:, :], RMS_EPS).then_inc(s_cst, 1)
            gp.memset(epsl[:, :], LN_EPS).then_inc(s_cst, 1)
            gp.memset(Bm[:, :, :, :], 0.0).then_inc(s_cst, 1)
            gp.memset(below[:, :], 1.0).then_inc(s_cst, 1)
            pool.wait_ge(s_cst, 8)
            gp.affine_select(out=below[:, :], in_=below[:, :], compare_op=ALU.is_ge, fill=0.0,
                             base=-1, pattern=[[1, P]], channel_multiplier=-1).then_inc(s_cst, 1)
            gp.iota(im8[:, :, :], pattern=[[0, 2], [1, NE]], base=-NE, channel_multiplier=0,
                    allow_small_or_imprecise_dtypes=True).then_inc(s_cst, 1)
            gp.iota(part0[:, :], pattern=[[T, NE]], base=0, channel_multiplier=0,
                    allow_small_or_imprecise_dtypes=True).then_inc(s_cst, 1)
            gp.iota(cnt[:, 0, :], pattern=[[T, NE]], base=0, channel_multiplier=0,
                    allow_small_or_imprecise_dtypes=True).then_inc(s_cst, 1)
            gp.iota(iotaR[:, :, :], pattern=[[1, NR + 1], [0, NE]], base=0, channel_multiplier=0,
                    allow_small_or_imprecise_dtypes=True).then_inc(s_cst, 1)
            gp.iota(hid[:, :, P:RW], pattern=[[2 * P, NT], [0, RW - P]], base=0, channel_multiplier=2,
                    allow_small_or_imprecise_dtypes=True).then_inc(s_cst, 1)
            gp.memset(one16[:, :], 1.0).then_inc(s_cst, 1)
            def add_log(q):
                w = slice(q * 512, (q + 1) * 512)
                pool.wait_ge(s_mx, q + 1)
                pool.wait_ge(s_abs, q + 9)
                gp.tensor_tensor(dt[:, w], dt[:, w], sc2[:, w], ALU.add).then_inc(s_dt, 1)

            def add_next(q):
                w0, w1 = q * 512, (q + 1) * 512
                pool.wait_ge(s_dt, q + 1)
                gp.tensor_copy(sc1[:, w1 - 1:w1], dt[:, w1 - 1:w1]).then_inc(s_gs, 1)
                gp.tensor_tensor(sc1[:, w0:w1 - 1], dt[:, w0:w1 - 1], dt[:, w0 + 1:w1], ALU.add).then_inc(s_gs, 1)

            add_log(0)
            for q in range(1, 4):
                add_log(q)
                add_next(q - 1)
            add_next(3)

            def rotate(b):
                pool.wait_ge(s_uv, 2 * b + 2)
                if not isinstance(b, int) or b > 0:
                    pool.wait_ge(s_S, b)
                    pool.wait_ge(s_bm, 4 * b)
                gp.tensor_tensor(R[:, 0::2, :], U[:, 0::2, :], V[:, 1::2, :], ALU.subtract).then_inc(s_rope, 1)
                gp.tensor_tensor(R[:, 1::2, :], V[:, 0::2, :], U[:, 1::2, :], ALU.add).then_inc(s_rope, 1)

            def distances(b):
                for j in range(2):
                    if j == 1:
                        pool.wait_ge(s_D, 2 * b + 2)
                    elif not isinstance(b, int) or b > 0:
                        pool.wait_ge(s_Em, 2 * b)
                    else:
                        pool.wait_ge(s_rat, 5)
                    gp.tensor_tensor(DI0[:, j, :, :], ident[:, :].rearrange("p (o t) -> p o t", o=1).broadcast_to([P, H, P]),
                                     nratio[:, bass.ds(2 * b + j, 1), :].rearrange("p o h -> p h o").broadcast_to([P, H, P]),
                                     ALU.mult).then_inc(s_di, 1)
                for j in range(2):
                    gp.affine_select(out=D[:, :, 2 * j, :], in_=D[:, :, 2 * j, :], compare_op=ALU.is_ge,
                                     fill=FAR, base=0, pattern=[[0, H], [1, P]],
                                     channel_multiplier=-1).then_inc(s_Dm, 1)

            def diagonal(b):
                pool.wait_ge(s_E, 4 * b + 4)
                pool.wait_ge(s_di, 2 * b + 2)
                for j in range(2):
                    gp.tensor_tensor(E[:, :, 2 * j, :], E[:, :, 2 * j, :], DI0[:, j, :, :],
                                     ALU.subtract).then_inc(s_Em, 1)

            def rms_rows(b):
                pool.wait_ge(s_ssq, 2 * b + 2)
                if not isinstance(b, int) or b > 0:
                    pool.wait_ge(s_x1p, 2 * b)
                gp.tensor_tensor(rms[:, :], ssq[:, :], epsr[:, :], ALU.add).then_inc(s_rm, 1)
                pool.wait_ge(s_rm, 2 * b + 1)
                gp.tensor_tensor(rms[:, :], rms[:, :], half[:, 0:2], ALU.pow).then_inc(s_rm, 1)

            def ln_rows(b):
                pool.wait_ge(s_mv, 2 * b + 2)
                if not isinstance(b, int) or b > 0:
                    pool.wait_ge(s_x1, 2 * b)
                gp.tensor_tensor(rstd[:, :], mv[:, :, 1], epsl[:, 0:2], ALU.add).then_inc(s_rstd, 1)
                pool.wait_ge(s_rstd, 2 * b + 1)
                gp.tensor_tensor(rstd[:, :], rstd[:, :], half[:, 0:2], ALU.pow).then_inc(s_rstd, 1)

            def low_part(b):
                pool.wait_ge(s_x1h, b + 1)
                gp.tensor_tensor(x1l[:, bass.ts(b, L)], x1Tb[:, :], x1h[:, bass.ts(b, L)], ALU.subtract).then_inc(s_x1l, 1)

            def wait_for_dma(signal, count):
                if not isinstance(count, int):
                    count = pool.snap(count)
                    pool.wait_ge(s_cst, 14)
                pool.wait_ge(signal, count)

            def route_rows(b):
                if isinstance(b, int) and b == 0:
                    pool.wait_ge(s_fill, 16 * (NROW // (P * FILL)))
                pool.wait_ge(s_rows, 2 * b + 2)
                pool.wait_ge(s_pos, NPOS * (b + 1))
                r1 = rows[:, slot(b), 1, :, P:RW]
                gp.tensor_tensor(r1, r1, ones[:, 0:2 * (RW - P)].rearrange("p (j f) -> p j f", j=2),
                                 ALU.add).then_inc(s_row1, 1)
                wait_for_dma(s_row1, b + 1)
                for c in range(2):
                    for j in range(2):
                        gp.indirect_dma_start(
                            out=xg, out_offset=bass.IndirectOffsetOnAxis(ap=posu[:, slot(b), 2 * c + j:2 * c + j + 1], axis=0),
                            in_=rows[:, slot(b), c, j, :], in_offset=None).then_inc(s_xg, 16)

            def step(k):
                if live(k, -1):
                    rms_rows(k - 1)
                if live(k, 1):
                    rotate(k + 1)
                if live(k, -1):
                    ln_rows(k - 1)
                if live(k, 1):
                    distances(k + 1)
                if live(k, 1):
                    diagonal(k + 1)
                if live(k, -1):
                    low_part(k - 1)
                if live(k, -3):
                    route_rows(k - 3)

            def unit(n, par):
                if routed(n):
                    r = n - NS0
                    pool.wait_ge(s_y, n + 1)
                    if not isinstance(r, int) or r > 0:
                        pool.wait_ge(s_carry, r)
                    gp.tensor_tensor(carry[:, :], ones[:, 0:2], ones[:, 0:2], ALU.mult).then_inc(s_carry, 1)
                    for s in range(2):
                        gp.indirect_dma_start(
                            out=yk, out_offset=bass.IndirectOffsetOnAxis(ap=idc[:, par, s:s + 1], axis=0),
                            in_=yr[:, par, s, :], in_offset=None,
                            bounds_check=2 * T - 1, oob_is_err=False).then_inc(s_yk[par], 16)
                else:
                    i = shared_index(n)
                    pool.wait_ge(s_y, n + 1)
                    gp.tensor_tensor(acc[:, 2 * i:2 * i + 2, :], acc[:, 2 * i:2 * i + 2, :], hid[:, 2 * i:2 * i + 2, 0:P],
                                     ALU.add).then_inc(s_ax, 1)

            steps(pool, step)
            rms_rows(NSEQ - 1)
            ln_rows(NSEQ - 1)
            route_rows(NSEQ - 3)
            route_rows(NSEQ - 2)
            low_part(NSEQ - 1)
            route_rows(NSEQ - 1)

            for n in range(EARLY):
                unit(n, n % 2)
            units(pool, unit)

            def weigh_second(c):
                pool.wait_ge(s_wk, 9)
                if c > 1:
                    pool.wait_ge(s_c, 2 * (c - 1))
                pool.wait_ge(s_ytk[c], 16)
                gp.tensor_tensor(wy2[:, c % 2, :, :], ytk[c][:, :, 1, :],
                                 wk[:, 7, 4 * c:4 * c + 4].rearrange("p (n o) -> p n o", o=1).broadcast_to([P, 4, P]),
                                 ALU.mult).then_inc(s_wy2, 1)

            weigh_second(0)
            for c in range(NCH):
                if c + 1 < NCH:
                    weigh_second(c + 1)
                w = slice(4 * c, 4 * c + 4)
                pool.wait_ge(s_fmv, 4 * c + 4)
                gp.tensor_tensor(frs[:, w], fmv[:, w, 1], epsl[:, :], ALU.add).then_inc(s_frs, 1)
                pool.wait_ge(s_frs, 2 * c + 1)
                gp.tensor_tensor(frs[:, w], frs[:, w], half[:, :], ALU.pow).then_inc(s_frs, 1)

        @block.scalar
        def _(act):
            ac = nc.scalar
            act.dma_start(wdt[:, :], w_dt).then_inc(s_wdt, 16)
            act.dma_start(vecs[:, 0:8 + 2 * NE], vectors).then_inc(s_vec, 16)
            act.dma_start(win[:, :], w_in).then_inc(s_w, 16)
            act.dma_start(wout[:, :, :], w_out.rearrange("(c p) d -> p c d", p=P)).then_inc(s_rw, 16)
            act.dma_start(b1a[:, :, :], b1).then_inc(s_rw, 16)
            act.dma_start(b2a[:, :, :], b2).then_inc(s_rw, 16)
            act.wait_ge(s_vec, 16)
            ac.activation(expA[:, :], vecs[:, 2:6], ACT.Exp).then_inc(s_A, 1)
            for q in range(4):
                w = slice(q * 512, (q + 1) * 512)
                act.wait_ge(s_dtp, q + 1)
                ac.activation(sc1[:, w], dtb[:, w], ACT.Abs, bias=vecs[:, 0:1]).then_inc(s_abs, 1)
                act.wait_ge(s_abs, 2 * q + 1)
                ac.activation(sc2[:, w], sc1[:, w], ACT.Exp, scale=-1.0).then_inc(s_abs, 1)
            for q in range(4):
                w = slice(q * 512, (q + 1) * 512)
                act.wait_ge(s_abs, 2 * q + 2)
                ac.activation(sc2[:, w], sc2[:, w], ACT.Ln, bias=1.0).then_inc(s_abs, 1)
            act.wait_ge(s_hTc, 4)
            ac.copy(hTb[:, :], hidT[:, 0:L]).then_inc(s_hTb, 1)
            act.wait_ge(s_Aneg, 2)
            for q in range(4):
                w = slice(q * 512, (q + 1) * 512)
                act.wait_ge(s_tab, 3 * q + 3)
                ac.activation(sinT[:, w], sc2[:, w], ACT.Sin, scale=-TURN).then_inc(s_sin, 1)
                ac.activation(cosT[:, w], sc2[:, w], ACT.Abs).then_inc(s_absr, 1)
                act.wait_ge(s_absr, q + 1)
                ac.activation(cosT[:, w], cosT[:, w], ACT.Sin, scale=-TURN, bias=half_pi[:, 0:1]).then_inc(s_cos, 1)
            act.wait_ge(s_rw, 48)
            ac.mul(b2p[:, :, 0, :], b2a[:, :, :], WS).then_inc(s_b2, 1)

            def next_tile(b):
                if not isinstance(b, int) or b > 0:
                    act.wait_ge(s_zx, 2 * b)
                ac.copy(hTb[:, :], hidT[:, bass.ts(b, L)]).then_inc(s_hTb, 1)

            def gate(b, j):
                act.wait_ge(s_zx, 2 * b + j + 1)
                if not isinstance(b, int) or b > 0:
                    act.wait_ge(s_sz, 2 * b + j - 1)
                ac.activation(th[:, j, :], Zb[:, 0:DI], ACT.Tanh, scale=0.5).then_inc(s_th, 1)

            def mask(b):
                act.wait_ge(s_rope, 2 * b + 2)
                if not isinstance(b, int) or b > 0:
                    act.wait_ge(s_S, b)
                else:
                    act.wait_ge(s_cst, 7)
                for h in range(H):
                    rows = slice(HALF * h, HALF * h + HALF)
                    ac.copy(Bm[rows, h, :, :], R[rows, 0:2, :]).then_inc(s_bm, 1)

            def exponentials(b):
                act.wait_ge(s_Dm, 2 * b + 2)
                if not isinstance(b, int) or b > 0:
                    act.wait_ge(s_P, 2 * b)
                for h in range(H):
                    ac.activation(E[:, h, :, :], D[:, h, :, :], ACT.Exp, scale=vecs[:, 2 + h:3 + h]).then_inc(s_E, 1)

            def squares(b):
                act.wait_ge(s_yg, b + 1)
                if not isinstance(b, int) or b > 0:
                    act.wait_ge(s_rm, 2 * b)
                for j in range(2):
                    ac.activation(sq[:, :], yg[:, j, :], ACT.Square, scale=DI ** -0.5, accum_out=ssq[:, j:j + 1]).then_inc(s_ssq, 1)
                    act.wait_ge(s_ssq, 2 * b + j + 1)

            def copy_yT(b):
                act.wait_ge(s_yT, b + 1)
                ac.copy(yT[:, :, :, :].rearrange("p j c t -> p (j c t)"), Mb).then_inc(s_yTc, 1)

            def copy_x1T(b):
                act.wait_ge(s_x1T, b + 1)
                if not isinstance(b, int) or b > 0:
                    act.wait_ge(s_x1l, b)
                ac.copy(x1Tb[:, :], Mb[:, 0:L]).then_inc(s_x1Tb, 1)
                act.wait_ge(s_x1Tb, b + 1)
                ac.copy(x1h[:, bass.ts(b, L)], x1Tb[:, :]).then_inc(s_x1h, 1)

            def keep_rows(b):
                act.wait_ge(s_x1, 2 * b + 2)
                ac.copy(hid[:, bass.ds(2 * b, 2), 0:P], x1[:, :, :]).then_inc(s_xrow, 1)

            def lay_rows(b):
                act.wait_ge(s_xrow, b + 1)
                if isinstance(b, int) and b == 0:
                    act.wait_ge(s_cst, 14)
                elif slot(b) == 0:
                    act.wait_ge(s_xg, 64 * b)
                for c in range(2):
                    ac.copy(rows[:, slot(b), c, :, :], hid[:, bass.ds(2 * b, 2), :]).then_inc(s_rows, 1)

            def split_high(e):
                act.wait_ge(s_A, 1)
                act.wait_ge(s_we, 32 * e + 32)
                dst1 = ws1[:, 0, :] if is_shared(e) else w1h[:, bass.ds(e, 1), :].rearrange("p o f -> p (o f)")
                raw1 = w1r[:, bass.ds(e % 2, 1), :].rearrange("p o f -> p (o f)")
                raw2 = w2r[:, bass.ds(e % 2, 1), :].rearrange("p o (c d) -> p (o c) d", c=FC)
                ac.mul(dst1, raw1, WS).then_inc(s_wh, 1)
                ac.mul(w2p[:, bass.ds(e, 1), :, 0, :].rearrange("p o c d -> p (o c) d"), raw2, WS).then_inc(s_wh, 1)

            def step(k):
                if live(k, -1):
                    squares(k - 1)
                if live(k, -1):
                    copy_yT(k - 1)
                if live(k, 1):
                    gate(k + 1, 0)
                if live(k, 1):
                    mask(k + 1)
                if live(k, 1):
                    gate(k + 1, 1)
                if live(k, 2):
                    next_tile(k + 2)
                if live(k, -1):
                    copy_x1T(k - 1)
                if live(k, 1):
                    exponentials(k + 1)
                if live(k, -3):
                    lay_rows(k - 3)
                if live(k, -1):
                    keep_rows(k - 1)
                if live(k, 1) or k == NE - 1:
                    split_high(k + 1)

            def x_high(n, par):
                r = n - NS0
                if isinstance(r, int) and r == 0:
                    act.wait_ge(s_tb, 13)
                if not isinstance(r, int) or r > 1:
                    act.wait_ge(s_g, 4 * n - 4)
                e = act.value_load(tabs[0:1, 0, bass.ds(r, 1)], min_val=0, max_val=NE - 1)
                ac.copy(bcur[:, par, :], b1a[:, bass.ds(e, 1), :].rearrange("p o f -> p (o f)")).then_inc(s_bc1, 1)
                act.wait_ge(s_turn, r + 1)
                if not isinstance(r, int) or r > 1:
                    act.wait_ge(s_h, 2 * n - 2)
                ac.copy(xh[:, par, :], ps[:, 6 + par, 0:TS]).then_inc(s_xh, 1)

            def gelu(n, par):
                for f in range(FC):
                    if f == 0 and (not isinstance(n, int) or n > 1):
                        act.wait_ge(s_gl, 2 * n - 2)
                    if f == 0 and routed(n):
                        act.wait_ge(s_bc1, n - NS0 + 1)
                    if f % 2 == 0:
                        act.wait_ge(s_h, 2 * n + f // 2 + 1)
                    bias = bcur[:, par, f:f + 1] if routed(n) else b1a[:, NE, f:f + 1]
                    ac.activation(g[:, par, f * TS:(f + 1) * TS], ps[:, 2 * par + f // 2, (f % 2) * TS:(f % 2 + 1) * TS],
                                  ACT.Gelu, scale=1.0 / WS, bias=bias).then_inc(s_g, 1)

            def low_half(n, par):
                act.wait_ge(s_O, n + 1)
                if not isinstance(n, int) or n > 1:
                    act.wait_ge(s_y, n - 1)
                ac.mul(tmp[:, par, :, :], Ob[par][:, :, 1, :], 1.0 / WS).then_inc(s_ob, 1)


            def unit(n, par):
                if has(n + 3) and routed(n + 3):
                    x_high(n + 3, 1 - par)
                if has(n + 2):
                    gelu(n + 2, par)
                low_half(n, par)

            act.wait_ge(s_tkc, 12)
            steps(act, step)
            squares(NSEQ - 1)
            lay_rows(NSEQ - 3)
            copy_yT(NSEQ - 1)
            lay_rows(NSEQ - 2)
            gelu(0, 0)
            copy_x1T(NSEQ - 1)
            keep_rows(NSEQ - 1)
            lay_rows(NSEQ - 1)
            gelu(1, 1)

            act.wait_ge(s_sel, NSEL * NSEQ)
            ac.activation(ex[:, :, :], dall[:, :, :], ACT.Exp).then_inc(s_ex, 1)
            ac.activation(wk[:, 0, :], r2all[:, :], ACT.Exp).then_inc(s_ex, 1)

            for n in range(EARLY):
                unit(n, n % 2)
            units(act, unit)

            def weigh_first(c):
                act.wait_ge(s_wk, 9)
                if c > 1:
                    act.wait_ge(s_c, 2 * (c - 1))
                act.wait_ge(s_ytk[c], 16)
                for q in range(4):
                    t = 4 * c + q
                    ac.mul(wy1[:, c % 2, q, :], ytk[c][:, q, 0, :], wk[:, 4, t:t + 1]).then_inc(s_wy1, 1)

            weigh_first(0)
            weigh_first(1)
            for c in range(NCH):
                if c + 2 < NCH:
                    weigh_first(c + 2)
                act.wait_ge(s_fnm, c + 1)
                for t in range(4 * c, 4 * c + 4):
                    ac.activation(acc[:, t, :], acc[:, t, :], ACT.Identity, scale=frs[:, t:t + 1],
                                  bias=fnm[:, t:t + 1]).then_inc(s_fin, 1)

        @block.vector
        def _(dve):
            v = nc.vector
            for q in range(4):
                dve.wait_ge(s_hT, q + 1)
                v.tensor_copy(hidT[:, 512 * q:512 * q + 512], ps[:, q, :]).then_inc(s_hTc, 1)
            dve.wait_ge(s_vec, 16)
            dve.wait_ge(s_A, 1)
            v.tensor_scalar(vecs[:, 2:6], expA[:, :], -1.0, None, ALU.mult).then_inc(s_Aneg, 1)
            v.memset(half_pi[:, :], float(np.pi / 2)).then_inc(s_Aneg, 1)
            def keep_columns(q):
                for n, dst in enumerate((dtK, cumK, gK)):
                    m = 3 * q + n
                    dve.wait_ge(s_tk, m + 1)
                    v.tensor_copy(dst[:, 4 * q:4 * q + 4, :],
                                  ps[:, m % 4, :].rearrange("p (n h i) -> p n h i", h=H, i=HALF)[:, :, :, 0]).then_inc(s_tkc, 1)

            for q in range(4):
                w = slice(q * 512, (q + 1) * 512)
                dve.wait_ge(s_abs, 2 * q + 1)
                v.tensor_scalar(dt[:, w], dtb[:, w], vecs[:, 0:1], 0.0, ALU.add, ALU.max).then_inc(s_mx, 1)
            dve.wait_ge(s_rw, 48)
            for c in range(2):
                v.tensor_scalar(wout[:, c, :], wout[:, c, :], vecs[:, 6 + c:7 + c], None, ALU.mult).then_inc(s_wo, 1)
            dve.wait_ge(s_cst, 3)
            for q in range(4):
                w = slice(q * 512, (q + 1) * 512)
                if q > 0:
                    keep_columns(q - 1)
                dve.wait_ge(s_dt, q + 1)
                for b in (2 * q, 2 * q + 1):
                    wb = slice(b * L, (b + 1) * L)
                    v.tensor_tensor_scan(cum[:, wb], ones[:, :], dt[:, wb], 0.0, ALU.mult, ALU.add).then_inc(s_cum, 1)
                dve.wait_ge(s_cum, 2 * q + 2)
                v.tensor_scalar(sinT[:, w], cum[:, w], vecs[:, 1:2], float(1 / (2 * np.pi)), ALU.mult, ALU.mult).then_inc(s_tab, 1)
                dve.wait_ge(s_tab, 3 * q + 1)
                v.tensor_scalar(cosT[:, w], sinT[:, w], MAGIC, None, ALU.add).then_inc(s_tab, 1)
                dve.wait_ge(s_tab, 3 * q + 2)
                v.scalar_tensor_tensor(out=sc2[:, w], in0=cosT[:, w], scalar=MAGIC, in1=sinT[:, w],
                                       op0=ALU.subtract, op1=ALU.subtract).then_inc(s_tab, 1)
            keep_columns(3)
            dve.wait_ge(s_tkc, 12)
            v.tensor_scalar(gK[:, :, :], gK[:, :, :], 1e-30, None, ALU.max).then_inc(s_rat, 1)
            dve.wait_ge(s_rat, 1)
            v.tensor_scalar(gx[:, :, :], gK[:, :, :], 0.25, None, ALU.mult).then_inc(s_rat, 1)
            v.reciprocal(nratio[:, :, :], gK[:, :, :]).then_inc(s_rat, 1)
            dve.wait_ge(s_rat, 3)
            v.tensor_tensor(nratio[:, :, :], nratio[:, :, :], dtK[:, :, :], ALU.mult).then_inc(s_rat, 1)
            dve.wait_ge(s_rat, 4)
            v.tensor_scalar(nratio[:, :, :], nratio[:, :, :], -1.0, 1.0, ALU.mult, ALU.add).then_inc(s_rat, 1)

            def bcast(ap, n):
                return ap.rearrange("p o h -> p h o").broadcast_to([P, H, n])

            def gate(b, j):
                ring = 2 * (b % 2)
                dve.wait_ge(s_th, 2 * b + j + 1)
                if not isinstance(b, int) or b > 1:
                    dve.wait_ge(s_pv, b - 1)
                    dve.wait_ge(s_yg, b - 1)
                v.tensor_tensor(xs[:, bass.ds(ring + j, 1), :].rearrange("p o (h d) -> p (o h) d", h=H),
                                Zb[:, DI:2 * DI].rearrange("p (h d) -> p h d", h=H),
                                bcast(gx[:, bass.ds(2 * b + j, 1), :], HD), ALU.mult).then_inc(s_xs, 1)
                v.scalar_tensor_tensor(out=szr[:, bass.ds(ring + j, 1), :].rearrange("p o d -> p (o d)"),
                                       in0=th[:, j, :], scalar=1.0,
                                       in1=Zb[:, 0:DI], op0=ALU.add, op1=ALU.mult).then_inc(s_sz, 1)

            def turn(b):
                dve.wait_ge(s_bc, b + 1)
                if not isinstance(b, int) or b > 0:
                    dve.wait_ge(s_rope, 2 * b)
                else:
                    dve.wait_ge(s_cos, 4)
                    dve.wait_ge(s_sin, 4)
                for tab, dst in ((cosT, U), (sinT, V)):
                    v.tensor_tensor(dst[:, :, :], BCb, tab[:, bass.ts(b, L)].rearrange("p (o t) -> p o t", o=1)
                                    .broadcast_to([P, 4, L]), ALU.mult).then_inc(s_uv, 1)

            def distances(b):
                dve.wait_ge(s_cb, b + 1)
                if not isinstance(b, int) or b > 0:
                    dve.wait_ge(s_E, 4 * b)
                v.tensor_tensor(D[:, :, 0:2, :].rearrange("p h a t -> p h (a t)"), S0b, bcast(cumK[:, bass.ds(2 * b, 1), :], L),
                                ALU.subtract).then_inc(s_D, 1)
                v.tensor_tensor(D[:, :, 2, :], S0b[:, :, P:L], bcast(cumK[:, bass.ds(2 * b + 1, 1), :], P),
                                ALU.subtract).then_inc(s_D, 1)

            def weigh(b):
                dve.wait_ge(s_S, b + 1)
                dve.wait_ge(s_Em, 2 * b + 2)
                if not isinstance(b, int) or b > 0:
                    dve.wait_ge(s_pv, b)
                else:
                    dve.wait_ge(s_fill, 16 * (NROW // (P * FILL)))
                v.tensor_tensor(Pm[:, :, 0:2, :].rearrange("p h a t -> p h (a t)"), S0b,
                                E[:, :, 0:2, :].rearrange("p h a t -> p h (a t)"), ALU.mult).then_inc(s_P, 1)
                v.tensor_tensor(Pm[:, :, 2, :], S1b, E[:, :, 2, :], ALU.mult).then_inc(s_P, 1)

            def gated(b):
                dve.wait_ge(s_pv, b + 1)
                dve.wait_ge(s_sz, 2 * b + 2)
                if not isinstance(b, int) or b > 0:
                    dve.wait_ge(s_yT, b)
                    dve.wait_ge(s_ssq, 2 * b)
                v.tensor_tensor(yg[:, :, :], Yb, szr[:, bass.ds(2 * (b % 2), 2), :], ALU.mult).then_inc(s_yg, 1)

            def norm(b):
                dve.wait_ge(s_o, b + 1)
                dve.wait_ge(s_rm, 2 * b + 2)
                for j in range(2):
                    v.scalar_tensor_tensor(out=x1p[:, j, :], in0=Mb[:, j * P:(j + 1) * P], scalar=rms[:, j:j + 1],
                                           in1=hid[:, bass.ds(2 * b + j, 1), 0:P].rearrange("p o d -> p (o d)"),
                                           op0=ALU.mult, op1=ALU.add).then_inc(s_x1p, 1)
                for j in range(2):
                    dve.wait_ge(s_x1p, 2 * b + j + 1)
                    v.bn_stats(st[:, j, :], x1p[:, j, :]).then_inc(s_st, 1)
                for j in range(2):
                    dve.wait_ge(s_rw, 48)
                    dve.wait_ge(s_st, 2 * b + j + 1)
                    v.bn_aggr(mv[:, j, :], st[:, j, :]).then_inc(s_mv, 1)

            def norm_out(b):
                dve.wait_ge(s_rstd, 2 * b + 2)
                if not isinstance(b, int) or b > 0:
                    dve.wait_ge(s_x1T, b)
                    dve.wait_ge(s_xrow, b)
                for j in range(2):
                    v.tensor_scalar(x1[:, j, :], x1p[:, j, :], mv[:, j, 0:1], rstd[:, j:j + 1],
                                    ALU.subtract, ALU.mult).then_inc(s_x1, 1)

            def keep_logits(b):
                dve.wait_ge(s_lg, b + 1)
                v.tensor_copy(LR[:, 0:2 * NE], Mb[:, L:L + 2 * NE]).then_inc(s_lgc, 1)

            def positions(b):
                dve.wait_ge(s_rk, b + 1)
                v.tensor_copy(LR[:, 2 * NE:6 * NE], ps[:, 6, 0:4 * NE]).then_inc(s_rkc, 1)
                dve.wait_ge(s_rkc, b + 1)
                if isinstance(b, int) and b == 0:
                    dve.wait_ge(s_cst, 14)
                else:
                    dve.wait_ge(s_pos, NPOS * b)
                n = NPOS * b
                v.tensor_tensor(pos[:, 0, :], LR[:, 2 * NE:3 * NE], cnt[:, 0, :], ALU.add).then_inc(s_pos, 1)
                v.tensor_tensor(cnt[:, 1, :], LR[:, 4 * NE:5 * NE], cnt[:, 0, :], ALU.add).then_inc(s_pos, 1)
                dve.wait_ge(s_pos, n + 2)
                v.tensor_tensor(pos[:, 1, :], LR[:, 3 * NE:4 * NE], cnt[:, 1, :], ALU.add).then_inc(s_pos, 1)
                v.tensor_tensor(cnt[:, 0, :], LR[:, 5 * NE:6 * NE], cnt[:, 1, :], ALU.add).then_inc(s_pos, 1)
                dve.wait_ge(s_pos, n + 3)
                v.tensor_tensor(pq[:, :, :, :], o12[:, :, :, :], pos[:, :, :].rearrange("p (o j) e -> p o j e", o=1)
                                .broadcast_to([P, 2, 2, NE]), ALU.mult).then_inc(s_pos, 1)
                dve.wait_ge(s_pos, n + 5)
                v.tensor_reduce(pf[:, :], pq[:, :, :, :].rearrange("p c j e -> p (c j) e"), AX_X, ALU.add).then_inc(s_pos, 1)

            def give_positions(b):
                dve.wait_ge(s_pos, NPOS * b + 6)
                if not isinstance(b, int) or (b > 0 and slot(b) == 0):
                    dve.wait_ge(s_xg, 64 * b)
                v.tensor_copy(posu[:, slot(b), :], pf[:, :]).then_inc(s_pos, 1)

            def row2(i):
                return rr[:, i, :].rearrange("p (j o) -> p j o", o=1).broadcast_to([P, 2, NE])

            def choose(b):
                n = NSEL * b
                dve.wait_ge(s_lgc, b + 1)
                v.tensor_tensor(lg[:, :, :], LR[:, 0:2 * NE].rearrange("p (j e) -> p j e", j=2),
                                rb[:, :].rearrange("p (o e) -> p o e", o=1).broadcast_to([P, 2, NE]), ALU.add).then_inc(s_sel, 1)
                dve.wait_ge(s_sel, n + 1)
                v.tensor_reduce(rr[:, 0, :], lg[:, :, :], AX_X, ALU.max).then_inc(s_sel, 1)
                dve.wait_ge(s_sel, n + 2)
                v.tensor_tensor(dS[:, :, :], lg[:, :, :], row2(0), ALU.subtract).then_inc(s_sel, 1)
                dve.wait_ge(s_sel, n + 3)
                v.scalar_tensor_tensor(out=q1[:, :, :], in0=dS[:, :, :], scalar=0.0, in1=im8[:, :, :],
                                       op0=ALU.is_equal, op1=ALU.mult).then_inc(s_sel, 1)
                dve.wait_ge(s_sel, n + 4)
                v.tensor_reduce(rr[:, 1, :], q1[:, :, :], AX_X, ALU.min).then_inc(s_sel, 1)
                dve.wait_ge(s_sel, n + 5)
                v.tensor_tensor(o12[:, 0, :, :], im8[:, :, :], row2(1), ALU.is_equal).then_inc(s_sel, 1)
                dve.wait_ge(s_sel, n + 6)
                v.scalar_tensor_tensor(out=d2[:, :, :], in0=o12[:, 0, :, :], scalar=-3e38, in1=dS[:, :, :],
                                       op0=ALU.mult, op1=ALU.add).then_inc(s_sel, 1)
                dve.wait_ge(s_sel, n + 7)
                v.tensor_reduce(rr[:, 2, :], d2[:, :, :], AX_X, ALU.max).then_inc(s_sel, 1)
                dve.wait_ge(s_sel, n + 8)
                v.tensor_tensor(q2[:, :, :], d2[:, :, :], row2(2), ALU.is_equal).then_inc(s_sel, 1)
                dve.wait_ge(s_sel, n + 9)
                v.tensor_tensor(q3[:, :, :], q2[:, :, :], im8[:, :, :], ALU.mult).then_inc(s_sel, 1)
                dve.wait_ge(s_sel, n + 10)
                v.tensor_reduce(rr[:, 3, :], q3[:, :, :], AX_X, ALU.min).then_inc(s_sel, 1)
                dve.wait_ge(s_sel, n + 11)
                v.tensor_tensor(o12[:, 1, :, :], im8[:, :, :], row2(3), ALU.is_equal).then_inc(s_sel, 1)
                dve.wait_ge(s_sel, n + 12)
                if not isinstance(b, int) or b > 0:
                    dve.wait_ge(s_rk, b)
                v.tensor_tensor(chosen[:, :, :], o12[:, 0, :, :], o12[:, 1, :, :], ALU.add).then_inc(s_sel, 1)
                v.tensor_copy(dall[:, bass.ds(2 * b, 2), :], dS[:, :, :]).then_inc(s_sel, 1)
                v.tensor_copy(r2all[:, bass.ds(2 * b, 2)], rr[:, 2, :]).then_inc(s_sel, 1)

            def split_low(e):
                dve.wait_ge(s_wh, 2 * e + 2)
                dst1 = ws1[:, 1, :] if is_shared(e) else w1l[:, bass.ds(e, 1), :].rearrange("p o f -> p (o f)")
                hi1 = ws1[:, 0, :] if is_shared(e) else w1h[:, bass.ds(e, 1), :].rearrange("p o f -> p (o f)")
                raw1 = w1r[:, bass.ds(e % 2, 1), :].rearrange("p o f -> p (o f)")
                raw2 = w2r[:, bass.ds(e % 2, 1), :].rearrange("p o (c d) -> p (o c) d", c=FC)
                w2e = w2p[:, bass.ds(e, 1), :, :, :].rearrange("p o c l d -> p (o c) l d")
                v.scalar_tensor_tensor(out=dst1, in0=raw1, scalar=WS, in1=hi1,
                                       op0=ALU.mult, op1=ALU.subtract).then_inc(s_wl, 1)
                v.scalar_tensor_tensor(out=w2e[:, :, 1, :], in0=raw2, scalar=WS, in1=w2e[:, :, 0, :],
                                       op0=ALU.mult, op1=ALU.subtract).then_inc(s_wl, 1)

            def step(k):
                if live(k, 1):
                    turn(k + 1)
                if live(k, -2):
                    keep_logits(k - 2)
                if live(k, 0):
                    weigh(k)
                if live(k, -3):
                    positions(k - 3)
                if live(k, 1):
                    gate(k + 1, 0)
                if live(k, -1):
                    norm(k - 1)
                if live(k, 1):
                    distances(k + 1)
                if live(k, -1):
                    norm_out(k - 1)
                if live(k, -3):
                    give_positions(k - 3)
                if live(k, -2):
                    choose(k - 2)
                if live(k, 0):
                    gated(k)
                if live(k, 1):
                    gate(k + 1, 1)
                if live(k, 0) or k == NE:
                    split_low(k)

            def x_low(n, par):
                r = n - NS0
                dve.wait_ge(s_xh, r + 1)
                if not isinstance(r, int) or r > 1:
                    dve.wait_ge(s_h, 2 * n - 2)
                v.tensor_tensor(xl[:, par, :], ps[:, 6 + par, 0:TS], xh[:, par, :], ALU.subtract).then_inc(s_xl, 1)
                v.tensor_copy(idall[:, bass.ds(r, 1), :].rearrange("p o s -> p (o s)"), xt[:, par, :, P]).then_inc(s_ida, 1)

            def low(n, par):
                for q in range(2):
                    w = slice(2 * q * TS, 2 * (q + 1) * TS)
                    if q == 0 and (not isinstance(n, int) or n > 1):
                        dve.wait_ge(s_O, n - 1)
                    dve.wait_ge(s_g, 4 * n + 2 * q + 2)
                    v.tensor_copy(gh[:, par, w], g[:, par, w]).then_inc(s_gh, 1)
                    dve.wait_ge(s_gh, 2 * n + q + 1)
                    v.tensor_tensor(gl[:, par, w], g[:, par, w], gh[:, par, w], ALU.subtract).then_inc(s_gl, 1)

            def result(n, par):
                if routed(n):
                    r = n - NS0
                    if not isinstance(r, int) or r > 1:
                        dve.wait_ge(s_yk[par], 16 * (r - par))
                    v.tensor_copy(idc[:, par, :], idall[:, bass.ds(r, 1), :].rearrange("p o s -> p (o s)")).then_inc(s_id2, 1)
                    dve.wait_ge(s_id2, r + 1)
                    dst = yr[:, par, :, :]
                else:
                    i = shared_index(n)
                    dst = acc[:, 2 * i:2 * i + 2, :]
                dve.wait_ge(s_ob, n + 1)
                v.scalar_tensor_tensor(out=dst, in0=Ob[par][:, :, 0, :], scalar=1.0 / WS, in1=tmp[:, par, :, :],
                                       op0=ALU.mult, op1=ALU.add).then_inc(s_y, 1)


            def unit(n, par):
                if has(n + 3) and routed(n + 3):
                    x_low(n + 3, 1 - par)
                if has(n + 2):
                    low(n + 2, par)
                result(n, par)

            dve.wait_ge(s_cst, 14)
            steps(dve, step)
            keep_logits(NSEQ - 2)
            positions(NSEQ - 3)
            give_positions(NSEQ - 3)
            split_low(NE)
            dve.wait_ge(s_b2, 1)
            v.scalar_tensor_tensor(out=b2p[:, :, 1, :], in0=b2a[:, :, :], scalar=WS, in1=b2p[:, :, 0, :],
                                   op0=ALU.mult, op1=ALU.subtract).then_inc(s_b2, 1)
            norm(NSEQ - 1)
            norm_out(NSEQ - 1)
            choose(NSEQ - 2)
            positions(NSEQ - 2)
            give_positions(NSEQ - 2)
            keep_logits(NSEQ - 1)
            choose(NSEQ - 1)
            dve.wait_ge(s_rope, 2 * NSEQ)
            low(0, 0)
            positions(NSEQ - 1)
            give_positions(NSEQ - 1)

            dve.wait_ge(s_pos, NPOS * NSEQ)
            v.tensor_tensor(tb[:, 0, :], cnt[:, 0, :], part0[:, :], ALU.subtract).then_inc(s_tb, 1)
            dve.wait_ge(s_tb, 1)
            v.tensor_scalar(tb[:, 1, :], tb[:, 0, :], 1.0 / TS, (TS - 1.0) / TS - 0.5 + 0.5 / TS, ALU.mult, ALU.add).then_inc(s_tb, 1)
            dve.wait_ge(s_tb, 2)
            v.tensor_scalar(tb[:, 2, :], tb[:, 1, :], MAGIC, None, ALU.add).then_inc(s_tb, 1)
            dve.wait_ge(s_tb, 3)
            v.tensor_scalar(tb[:, 3, :], tb[:, 2, :], MAGIC, None, ALU.subtract).then_inc(s_tb, 1)
            dve.wait_ge(s_tb, 4)
            v.tensor_tensor_scan(tb[:, 4, :], ones[:, 0:NE], tb[:, 3, :], 0.0, ALU.mult, ALU.add).then_inc(s_tb, 1)
            dve.wait_ge(s_tb, 5)
            m = NE - 1
            v.tensor_tensor(tg[:, :, 0:m], iotaR[:, :, 0:m],
                            tb[:, 4, 0:m].rearrange("p (o e) -> p o e", o=1).broadcast_to([P, NR + 1, m]), ALU.is_ge).then_inc(s_tb, 1)
            dve.wait_ge(s_tb, 6)
            v.tensor_reduce(tr[:, 0, :], tg[:, :, 0:m], AX_X, ALU.add).then_inc(s_tb, 1)
            v.tensor_tensor(tg2[:, :, 0:m], tg[:, :, 0:m],
                            tb[:, 3, 0:m].rearrange("p (o e) -> p o e", o=1).broadcast_to([P, NR + 1, m]), ALU.mult).then_inc(s_tb, 1)
            dve.wait_ge(s_tb, 8)
            v.tensor_reduce(tr[:, 1, :], tg2[:, :, 0:m], AX_X, ALU.add).then_inc(s_tb, 1)
            dve.wait_ge(s_tb, 9)
            v.tensor_tensor(tr[:, 2, :], iotaR[:, :, 0], tr[:, 1, :], ALU.subtract).then_inc(s_tb, 1)
            dve.wait_ge(s_tb, 10)
            v.tensor_scalar(tr[:, 3, :], tr[:, 2, :], float(T // TS), float(TS), ALU.min, ALU.mult).then_inc(s_tb, 1)
            dve.wait_ge(s_tb, 11)
            v.scalar_tensor_tensor(out=tabs[:, 1, :], in0=tr[:, 0, :], scalar=float(T), in1=tr[:, 3, :],
                                   op0=ALU.mult, op1=ALU.add).then_inc(s_tb, 1)
            v.tensor_copy(tabs[:, 0, :], tr[:, 0, :]).then_inc(s_tb, 1)

            low(1, 1)
            for n in range(EARLY):
                unit(n, n % 2)

            dve.wait_ge(s_ex, 2)
            v.tensor_reduce(wk[:, 1, :], ex[:, :, :], AX_X, ALU.add).then_inc(s_wk, 1)
            dve.wait_ge(s_wk, 1)
            v.reciprocal(wk[:, 2, :], wk[:, 1, :]).then_inc(s_wk, 1)
            dve.wait_ge(s_wk, 2)
            v.tensor_tensor(wk[:, 3, :], wk[:, 2, :], wk[:, 0, :], ALU.mult).then_inc(s_wk, 1)
            dve.wait_ge(s_wk, 3)
            v.tensor_tensor(wk[:, 4, :], wk[:, 2, :], wk[:, 3, :], ALU.add).then_inc(s_wk, 1)
            dve.wait_ge(s_wk, 4)
            v.tensor_scalar(wk[:, 5, :], wk[:, 4, :], 1e-9, None, ALU.add).then_inc(s_wk, 1)
            dve.wait_ge(s_wk, 5)
            v.reciprocal(wk[:, 6, :], wk[:, 5, :]).then_inc(s_wk, 1)
            dve.wait_ge(s_wk, 6)
            v.tensor_tensor(wk[:, 1, :], wk[:, 2, :], wk[:, 6, :], ALU.mult).then_inc(s_wk, 1)
            v.tensor_tensor(wk[:, 7, :], wk[:, 3, :], wk[:, 6, :], ALU.mult).then_inc(s_wk, 1)
            dve.wait_ge(s_wk, 8)
            v.tensor_copy(wk[:, 4, :], wk[:, 1, :]).then_inc(s_wk, 1)

            units(dve, unit)

            def combine(c):
                w = slice(4 * c, 4 * c + 4)
                dve.wait_ge(s_ax, 2 * c + 2)
                for n, (term, ready, count) in enumerate(((wy1, s_wy1, 4 * c + 4), (wy2, s_wy2, c + 1))):
                    dve.wait_ge(ready, count)
                    if n == 1:
                        dve.wait_ge(s_c, 2 * c + 1)
                    v.tensor_tensor(acc[:, w, :], acc[:, w, :], term[:, c % 2, :, :], ALU.add).then_inc(s_c, 1)
                dve.wait_ge(s_c, 2 * c + 2)
                for t in range(4 * c, 4 * c + 4):
                    v.bn_stats(fst[:, t, :], acc[:, t, :]).then_inc(s_fst, 1)
                for t in range(4 * c, 4 * c + 4):
                    dve.wait_ge(s_fst, t + 1)
                    v.bn_aggr(fmv[:, t, :], fst[:, t, :]).then_inc(s_fmv, 1)

            def shift(c):
                w = slice(4 * c, 4 * c + 4)
                dve.wait_ge(s_frs, 2 * c + 2)
                v.scalar_tensor_tensor(out=fnm[:, w], in0=fmv[:, w, 0], scalar=-1.0, in1=frs[:, w],
                                       op0=ALU.mult, op1=ALU.mult).then_inc(s_fnm, 1)

            for c in range(NCH):
                combine(c)
                if c > 0:
                    shift(c - 1)
            shift(NCH - 1)

        @block.tensor
        def _(pe):
            te = nc.tensor
            pe.wait_ge(s_id, 1)
            for q in range(4):
                pe.wait_ge(s_hid[q], 16)
                for j in range(4):
                    m = te.transpose(ps[:, q, j * P:(j + 1) * P], hid[:, 4 * q + j, 0:P], ident[:, :])
                m.then_inc(s_hT, 1)
            pe.wait_ge(s_wdt, 16)
            for q in range(4):
                pe.wait_ge(s_hTc, q + 1)
                te.matmul(ps[:, 4 + q, :], wdt[:, :], hidT[:, 512 * q:512 * q + 512], start=True,
                          stop=True).then_inc(s_dtp, 1)
            for q in range(4):
                for n, (src, ready, count) in enumerate(((dt, s_dt, q + 1), (cum, s_cum, 2 * q + 2), (sc1, s_gs, 2 * q + 2))):
                    bank = (3 * q + n) % 4
                    pe.wait_ge(ready, count)
                    if 3 * q + n > 3:
                        pe.wait_ge(s_tkc, 3 * q + n - 3)
                    for j in range(4):
                        t0 = (4 * q + j) * P
                        m = te.transpose(ps[:, bank, j * P:(j + 1) * P], src[:, t0:t0 + P], ident[:, :])
                    m.then_inc(s_tk, 1)

            def spread(b):
                if not isinstance(b, int) or b > 0:
                    pe.wait_ge(s_P, 2 * b)
                for h in range(H):
                    m = te.matmul(S0b[:, h, :], sel[:, h, :], cum[:, bass.ts(b, L)], start=True, stop=True)
                m.then_inc(s_cb, 1)

            def scores(b):
                pe.wait_ge(s_bm, 4 * b + 4)
                pe.wait_ge(s_rope, 2 * b + 2)
                pe.wait_ge(s_D, 2 * b + 2)
                for h in range(H):
                    for e in range(2):
                        te.matmul(S0b[:, h, :], Bm[:, h, e, 0:P], R[:, 2 + e, :], start=(e == 0), stop=(e == 1))
                for h in range(H):
                    for e in range(2):
                        m = te.matmul(S1b[:, h, :], Bm[:, h, e, P:L], R[:, 2 + e, P:L], start=(e == 0), stop=(e == 1))
                m.then_inc(s_S, 1)

            def project_zx(b, j):
                if j == 0:
                    pe.wait_ge(s_hTb, b + 1)
                if not isinstance(b, int) or b > 0 or j > 0:
                    pe.wait_ge(s_sz, 2 * b + j)
                te.matmul(Zb, hTb[:, j * P:(j + 1) * P], win[:, Z0:B0], start=True, stop=True).then_inc(s_zx, 1)

            def project_bc(b):
                if not isinstance(b, int) or b > 0:
                    pe.wait_ge(s_uv, 2 * b)
                for n, c0 in enumerate((B0, B0 + 1, C0, C0 + 1)):
                    m = te.matmul(BCb[:, n, :], win[:, c0:c0 + DI - 1:2], hidT[:, bass.ts(b, L)], start=True, stop=True)
                m.then_inc(s_bc, 1)

            def values(b):
                pe.wait_ge(s_P, 2 * b + 2)
                pe.wait_ge(s_xs, 2 * b + 2)
                if not isinstance(b, int) or b > 0:
                    pe.wait_ge(s_yg, b)
                if not isinstance(b, int) or b > 2:
                    pe.wait_ge(s_rkc, b - 2)
                ring = 2 * (b % 2)
                for h in range(H):
                    f = slice(h * HD, (h + 1) * HD)
                    x0 = xs[:, bass.ds(ring, 1), f].rearrange("p o d -> p (o d)")
                    x1_ = xs[:, bass.ds(ring + 1, 1), f].rearrange("p o d -> p (o d)")
                    te.matmul(Yb[:, 0, f], Pm[:, h, 0, :], x0, start=True, stop=True)
                    te.matmul(Yb[:, 1, f], Pm[:, h, 1, :], x0, start=True, stop=False)
                    m = te.matmul(Yb[:, 1, f], Pm[:, h, 2, :], x1_, start=False, stop=True)
                m.then_inc(s_pv, 1)

            def turn_y(b):
                pe.wait_ge(s_yg, b + 1)
                if not isinstance(b, int) or b > 0:
                    pe.wait_ge(s_lgc, b)
                for j in range(2):
                    for c in range(2):
                        n = 2 * j + c
                        m = te.transpose(Mb[:, n * P:(n + 1) * P], yg[:, j, c * P:(c + 1) * P], ident[:, :])
                m.then_inc(s_yT, 1)

            def project_out(b):
                pe.wait_ge(s_yTc, b + 1)
                if isinstance(b, int) and b == 0:
                    pe.wait_ge(s_wo, 2)
                for j in range(2):
                    for c in range(2):
                        m = te.matmul(Mb[:, j * P:(j + 1) * P], yT[:, j, c, :], wout[:, c, :], start=(c == 0), stop=(c == 1))
                m.then_inc(s_o, 1)

            def turn_x1(b):
                pe.wait_ge(s_x1, 2 * b + 2)
                for j in range(2):
                    m = te.transpose(Mb[:, j * P:(j + 1) * P], x1[:, j, :], ident[:, :])
                m.then_inc(s_x1T, 1)

            def route(b):
                pe.wait_ge(s_x1Tb, b + 1)
                for j in range(2):
                    m = te.matmul(Mb[:, L + j * NE:L + (j + 1) * NE], x1Tb[:, j * P:(j + 1) * P], rw[:, :], start=True, stop=True)
                m.then_inc(s_lg, 1)

            def rank(b):
                pe.wait_ge(s_yg, min(b + 3, NSEQ) if isinstance(b, int) else b + 3)
                if isinstance(b, int) and b == 0:
                    pe.wait_ge(s_cst, 9)
                pe.wait_ge(s_sel, NSEL * b + 13)
                if not isinstance(b, int) or b > 0:
                    pe.wait_ge(s_rkc, b)
                for n, lhsT in enumerate((below[:, :], ones[:, 0:P])):
                    m = te.matmul(ps[:, 6, 2 * n * NE:2 * (n + 1) * NE], lhsT, chosen[:, :, :].rearrange("p j e -> p (j e)"),
                                  start=True, stop=True)
                m.then_inc(s_rk, 1)

            def step(k):
                if live(k, 0):
                    scores(k)
                if live(k, -3):
                    rank(k - 3)
                if live(k, -1):
                    turn_y(k - 1)
                if live(k, 1):
                    project_zx(k + 1, 0)
                if live(k, -1):
                    project_out(k - 1)
                if live(k, 1):
                    spread(k + 1)
                if live(k, 0):
                    values(k)
                if live(k, 1):
                    project_zx(k + 1, 1)
                if live(k, -1):
                    turn_x1(k - 1)
                if live(k, 2):
                    project_bc(k + 2)
                if live(k, -1):
                    route(k - 1)

            def product(bank, ah, al, bh, bl):
                te.matmul(bank, ah, bh, start=True, stop=False)
                te.matmul(bank, ah, bl, start=False, stop=False)
                return te.matmul(bank, al, bh, start=False, stop=True)

            def expert(n):
                return pe.value_load(tabs[0:1, 0, bass.ds(n - NS0, 1)], min_val=0, max_val=NE - 1)

            def turn_rows(n, par):
                r = n - NS0
                if not isinstance(r, int) or r > 1:
                    pe.wait_ge(s_xl, r - 1)
                pe.wait_ge(s_xt[par], 8 * (r - par) + 16)
                for s in range(2):
                    m = te.transpose(ps[:, 6 + par, s * P:(s + 1) * P], xt[:, par, s, 0:P], ident[:, :])
                m.then_inc(s_turn, 1)

            def first(n, par, e=NE):
                if not isinstance(n, int) or n > 1:
                    pe.wait_ge(s_g, 4 * n - 4)
                if routed(n):
                    pe.wait_ge(s_xl, n - NS0 + 1)
                    x = xh[:, par, :], xl[:, par, :]
                else:
                    i = shared_index(n)
                    pe.wait_ge(s_x1l, i + 1)
                    x = x1h[:, i * TS:(i + 1) * TS], x1l[:, i * TS:(i + 1) * TS]
                for f in range(FC):
                    fs = slice(f * P, (f + 1) * P)
                    if routed(n):
                        wh, wl = (w[:, bass.ds(e, 1), fs].rearrange("p o f -> p (o f)") for w in (w1h, w1l))
                    else:
                        wh, wl = ws1[:, 0, fs], ws1[:, 1, fs]
                    m = product(ps[:, 2 * par + f // 2, (f % 2) * TS:(f % 2 + 1) * TS], wh, wl, *x)
                    if f % 2 == 1:
                        m.then_inc(s_h, 1)

            def second(n, par, e):
                if not isinstance(n, int) or n > 1:
                    pe.wait_ge(s_y, n - 1)
                w2e = w2p[:, bass.ds(e, 1), :, :, :].rearrange("p o c l d -> p (o c) (l d)")
                b2e = b2p[:, bass.ds(e, 1), :, :].rearrange("p o l d -> p (o l d)")
                for s in range(2):
                    both = Ob[par][:, s, :, :].rearrange("p l d -> p (l d)")
                    te.matmul(both, one16[:, :], b2e, start=True, stop=False)
                    for f in range(FC):
                        if s == 0 and f % 2 == 0:
                            pe.wait_ge(s_gl, 2 * n + f // 2 + 1)
                        c0 = f * TS + s * P
                        te.matmul(Ob[par][:, s, 0, :], gl[:, par, c0:c0 + P], w2e[:, f, 0:P], start=False, stop=False)
                        m = te.matmul(both, gh[:, par, c0:c0 + P], w2e[:, f, :], start=False, stop=(f == FC - 1))
                m.then_inc(s_O, 1)


            def look_up(n):
                return expert(n) if has(n) and routed(n) else NE

            def unit(n, par, e=None, e2=None):
                if e is None:
                    e, e2 = look_up(n), look_up(n + 2)
                if has(n + 2):
                    first(n + 2, par, e2)
                if has(n + 3) and routed(n + 3):
                    turn_rows(n + 3, 1 - par)
                second(n, par, e)

            pe.wait_ge(s_id, 2)
            pe.wait_ge(s_w, 16)
            pe.wait_ge(s_vec, 16)
            pe.wait_ge(s_tkc, 12)
            pe.wait_ge(s_mx, 4)
            project_bc(0)
            steps(pe, step)
            rank(NSEQ - 3)
            turn_y(NSEQ - 1)
            project_out(NSEQ - 1)
            pe.wait_ge(s_wl, 2 * NE + 2)
            pe.wait_ge(s_b2, 2)
            pe.wait_ge(s_cst, 15)
            first(0, 0)
            turn_x1(NSEQ - 1)
            rank(NSEQ - 2)
            route(NSEQ - 1)
            first(1, 1)
            rank(NSEQ - 1)

            for n in range(EARLY):
                unit(n, n % 2)
            for n in range(EARLY, LOOP0):
                unit(n, n % 2)
            with pe.Fori(LOOP0 // 2, LOOP1 // 2) as k:
                _, e = nc.values_load_multi_w_load_instructions(
                    tabs[0:1, 0, bass.ds(2 * k - NS0, 4)], engines=(mybir.EngineType.PE,), min_val=0, max_val=NE - 1)
                unit(2 * k, 0, e[0], e[2])
                unit(2 * k + 1, 1, e[1], e[3])
            for n in range(LOOP1, NU):
                unit(n, n % 2)


def live(k, off):
    return not isinstance(k, int) or 0 <= k + off < NSEQ


def steps(engine, step):
    for k in (-1, 0, 1, 2):
        step(k)
    with engine.Fori(3, NSEQ - 2) as k:
        step(k)
    for k in range(NSEQ - 2, NSEQ):
        step(k)


def slot(b):
    return max(0, b - (NSEQ - 4)) if isinstance(b, int) else 0


def is_shared(e):
    return isinstance(e, int) and e == NE


def routed(n):
    return not isinstance(n, int) or NS0 <= n < NS0 + NR


def has(n):
    return not isinstance(n, int) or n < NU


def shared_index(n):
    return n if n < NS0 else n - NR


def units(engine, unit):
    for n in range(EARLY, LOOP0):
        unit(n, n % 2)
    with engine.Fori(LOOP0 // 2, LOOP1 // 2) as k:
        for par in range(2):
            unit(2 * k + par, par)
    for n in range(LOOP1, NU):
        unit(n, n % 2)


def kernel(**inputs):
    import concourse.bacc as _bacc
    from concourse.bass_utils import run_bass_kernel_spmd as _run

    a = {k: np.asarray(v) for k, v in inputs.items()}
    at, ff = "L0_attn_", "L0_ffn_"
    w_in = a[at + "W_in"]
    half = np.arange(HALF, dtype=np.float32) / np.float32(HALF)
    inv = (np.float32(1.0) / np.power(np.float32(10000.0), half)).astype(np.float32)
    arrays = {
        "hidden": a[at + "hidden"].reshape(T, P),
        "w_in": w_in,
        "w_dt": np.repeat(w_in[:, DT0:DT0 + H], HALF, axis=1),
        "vectors": np.concatenate([
            np.repeat(a[at + "dt_bias"], HALF).reshape(P, 1),
            np.tile(inv, H).reshape(P, 1),
            np.broadcast_to(a[at + "A_log"][None, :], (P, H)),
            a[at + "norm_weight"].reshape(2, P).T,
            a[ff + "router_w"],
            np.broadcast_to(a[ff + "router_b"][None, :], (P, NE))], axis=1),
        "w_out": a[at + "W_out"],
        "w1": np.concatenate([a[ff + "exp_w1"], a[ff + "shared_w1"][None]], axis=0),
        "w2": np.concatenate([a[ff + "exp_w2"], a[ff + "shared_w2"][None]], axis=0),
        "b1": np.concatenate([a[ff + "exp_b1"], a[ff + "shared_b1"][None]], axis=0).reshape(NE + 1, FC, P).transpose(2, 0, 1),
        "b2": np.concatenate([a[ff + "exp_b2"], a[ff + "shared_b2"][None]], axis=0)[None],
    }
    nc = _bacc.Bacc("TRN2", target_bir_lowering=False, num_devices=1)
    feed, args = {}, []
    for name, x in arrays.items():
        x = np.ascontiguousarray(x)
        feed[f"in_{name}"] = x
        args.append(nc.dram_tensor(f"in_{name}", x.shape, mybir.dt.from_np(x.dtype), kind="ExternalInput").ap())
    xg = nc.dram_tensor("routed_rows", (NROW, RW), F32, kind="Internal").ap()
    yk = nc.dram_tensor("routed_results", (2 * T, P), F32, kind="Internal").ap()
    out = nc.dram_tensor("out_0", (T, P), F32, kind="ExternalOutput").ap()
    build(nc, *args, xg, yk, out)
    r = _run(nc, [feed], core_ids=[0])
    return r.results[0]["out_0"].reshape(NSEQ, L, P)
```
